# Optimizing a Trainium2 kernel written in Bass

```python
import numpy as np
import jax
import jax.numpy as jnp

def _softmax(x, axis=-1):
    return jax.nn.softmax(x, axis=axis)

def _gelu(x):
    return jax.nn.gelu(x, approximate=True)

def _silu(x):
    return jax.nn.silu(x)

def _sigmoid(x):
    return jax.nn.sigmoid(x)

def _layernorm(x, axis=-1, eps=1e-05):
    m = jnp.mean(x, axis=axis, keepdims=True)
    v = jnp.var(x, axis=axis, keepdims=True)
    return (x - m) / jnp.sqrt(v + eps)

def _scatter_add(tgt, idx, src, axis=0):
    return tgt.at[idx].add(src)

def _segment_sum(src, seg, n):
    return jax.ops.segment_sum(src, seg, n)
kernel_name = 'mk_adj_resnorm_d2_adj_r2_de4f29'

def setup_inputs(seed: int=0):
    np.random.seed(seed)
    _w = jnp.asarray

    def _rec_inputs():
        import jax
        import jax.numpy as jnp
        _gk = jax.random.key(seed)
        x = 7.34e-05 + 1 * jax.random.normal(jax.random.fold_in(_gk, 1), (64, 128, 256), jnp.float32)
        _a = jax.random.bernoulli(jax.random.fold_in(_gk, 2), 0.015625, (128, 128))
        _a = jnp.logical_or(_a, jnp.swapaxes(_a, -1, -2))
        _a = jnp.logical_or(_a, jnp.eye(128, dtype=bool))
        _af = _a.astype(jnp.float32)
        adj = _af
        return (x, adj)
    x, adj = _rec_inputs()

    def _L0_gnn_setup():
        import jax, jax.numpy as jnp
        import numpy as np
        B, N, D, H = (16, 1025, 256, 8)
        LN_EPS = 1e-05

        def _make_mask(key, n):
            n_proto = n - 1
            adj = jax.random.bernoulli(key, 0.03, (n_proto, n_proto)).astype(jnp.float32)
            adj = jnp.clip(adj + adj.T + jnp.eye(n_proto, dtype=jnp.float32), 0.0, 1.0)
            mask = jnp.zeros((n, n), dtype=jnp.float32)
            mask = mask.at[0, :].set(1.0).at[:, 0].set(1.0)
            mask = mask.at[1:, 1:].set(adj)
            return mask
        key = jax.random.key(seed)
        ks = jax.random.split(key, 7)
        s = 1.0 / np.sqrt(D)
        return {'x': jax.random.normal(ks[0], (B, N, D), dtype=jnp.float32), 'w_qkv': jax.random.uniform(ks[1], (D, 3 * D), dtype=jnp.float32, minval=-s, maxval=s), 'w_proj': jax.random.uniform(ks[2], (D, D), dtype=jnp.float32, minval=-s, maxval=s), 'b_proj': jnp.zeros((D,), dtype=jnp.float32), 'ln_gamma': jnp.ones((D,), dtype=jnp.float32), 'ln_beta': jnp.zeros((D,), dtype=jnp.float32), 'attn_mask': _make_mask(ks[3], N)}
    _L0_gnn_all = _L0_gnn_setup()
    _L0_gnn_in = {k: v for k, v in _L0_gnn_all.items() if k in ('w_qkv', 'w_proj', 'b_proj', 'ln_gamma', 'ln_beta')}
    del _L0_gnn_all

    def _L1_gnn_setup():
        import jax, jax.numpy as jnp
        import numpy as np
        B, N, D, O = (8, 2048, 256, 256)
        key = jax.random.key(seed)
        k1, k2, k3, k4 = jax.random.split(key, 4)
        x = jax.random.normal(k1, (B, N, D), dtype=jnp.float32)
        adj = jax.random.uniform(k2, (N, N), dtype=jnp.float32)
        weight = jax.random.normal(k3, (D, O), dtype=jnp.float32) * 0.02
        bias = jax.random.normal(k4, (O,), dtype=jnp.float32) * 0.02
        return {'x': x, 'adj': adj, 'weight': weight, 'bias': bias}
    _L1_gnn_all = _L1_gnn_setup()
    _L1_gnn_in = {k: v for k, v in _L1_gnn_all.items() if k in ('weight', 'bias')}
    del _L1_gnn_all
    return {'x': x, 'adj': adj, 'L0_gnn_w_qkv': _L0_gnn_in['w_qkv'], 'L0_gnn_w_proj': _L0_gnn_in['w_proj'], 'L0_gnn_b_proj': _L0_gnn_in['b_proj'], 'L0_gnn_ln_gamma': _L0_gnn_in['ln_gamma'], 'L0_gnn_ln_beta': _L0_gnn_in['ln_beta'], 'L1_gnn_weight': _L1_gnn_in['weight'], 'L1_gnn_bias': _L1_gnn_in['bias']}

def reference(x, adj, L0_gnn_w_qkv, L0_gnn_w_proj, L0_gnn_b_proj, L0_gnn_ln_gamma, L0_gnn_ln_beta, L1_gnn_weight, L1_gnn_bias):
    import jax
    import jax.numpy as jnp

    def _L0_gnn_ref(x, w_qkv, w_proj, b_proj, ln_gamma, ln_beta, attn_mask):
        import jax, jax.numpy as jnp
        import numpy as np
        B, N, D, H = (16, 1025, 256, 8)
        LN_EPS = 1e-05

        def _make_mask(key, n):
            n_proto = n - 1
            adj = jax.random.bernoulli(key, 0.03, (n_proto, n_proto)).astype(jnp.float32)
            adj = jnp.clip(adj + adj.T + jnp.eye(n_proto, dtype=jnp.float32), 0.0, 1.0)
            mask = jnp.zeros((n, n), dtype=jnp.float32)
            mask = mask.at[0, :].set(1.0).at[:, 0].set(1.0)
            mask = mask.at[1:, 1:].set(adj)
            return mask
        b, n, d = x.shape
        hd = d // H
        scale = hd ** (-0.5)
        qkv = (x @ w_qkv).reshape(b, n, 3, H, hd).transpose(2, 0, 3, 1, 4)
        q, k, v = (qkv[0], qkv[1], qkv[2])
        attn = jnp.einsum('bhnd,bhmd->bhnm', q, k) * scale
        attn = jnp.where(attn_mask[None, None] == 0, -jnp.inf, attn)
        attn = jax.nn.softmax(attn, axis=-1)
        o = jnp.einsum('bhnm,bhmd->bhnd', attn, v).transpose(0, 2, 1, 3).reshape(b, n, d)
        o = o @ w_proj + b_proj
        mu = jnp.mean(o, axis=-1, keepdims=True)
        var = jnp.mean(jnp.square(o - mu), axis=-1, keepdims=True)
        ln = (o - mu) * jax.lax.rsqrt(var + LN_EPS) * ln_gamma + ln_beta
        return o + ln

    def _L1_gnn_ref(x, adj, weight, bias):
        import jax, jax.numpy as jnp
        import numpy as np
        B, N, D, O = (8, 2048, 256, 256)
        y = jnp.einsum('nm,bmd->bnd', adj, x)
        out = jnp.einsum('bnd,do->bno', y, weight) + bias
        return out
    x = _layernorm(x + _L0_gnn_ref(x, L0_gnn_w_qkv, L0_gnn_w_proj, L0_gnn_b_proj, L0_gnn_ln_gamma, L0_gnn_ln_beta, adj), axis=-1)
    x = _layernorm(x + _L1_gnn_ref(x, adj, L1_gnn_weight, L1_gnn_bias), axis=-1)
    return x

_drawn_inputs = setup_inputs


def setup_inputs(seed=0):
    import zlib

    import numpy as np

    out = dict(_drawn_inputs(seed))
    spreads = {'L0_gnn_b_proj': (0.0, 0.1), 'L0_gnn_ln_gamma': (1.0, 0.2), 'L0_gnn_ln_beta': (0.0, 0.1)}
    factors = {'L1_gnn_bias': 4.446}
    for name, (base, spread) in spreads.items():
        noise = np.random.default_rng([zlib.crc32(name.encode()), seed]).standard_normal(out[name].shape)
        drawn = base * np.exp(spread * noise) if base else spread * noise
        out[name] = jnp.asarray(drawn.astype(out[name].dtype))
    for name, factor in factors.items():
        out[name] = (out[name] * factor).astype(out[name].dtype)
    return out
```

```python
import concourse.bass as bass
from concourse import mybir
from contextlib import ExitStack

F32 = mybir.dt.float32
F32R = mybir.dt.float32r
ALU = mybir.AluOpType
ACT = mybir.ActivationFunctionType


def gnn_block_kernel(nc, x, adj, w_qkv, w_proj, b_proj, gamma, beta, w_gnn, b_gnn, out):
    B, N, D = x.shape
    HD = 32
    H = D // HD
    KC = D // 128
    HC = H // KC
    PAIRS = B // 2
    SCALE = float(HD) ** -0.5
    EPS = 1e-5
    BLOCKED = 1e30
    HUGE = 3e38

    ctx = ExitStack()
    with ctx:
        def sb(name, shape, dt=F32):
            return ctx.enter_context(nc.sbuf_tensor(name, shape, dt))

        def bank(name):
            return ctx.enter_context(nc.psum_tensor(name, [128, 512], F32))

        def sem(name):
            return ctx.enter_context(nc.semaphore(name))

        wqkv = sb("wqkv", [128, KC, 3 * D])
        wqkv_hi = sb("wqkv_hi", [128, KC, 3 * D], F32R)
        wqkv_lo = sb("wqkv_lo", [128, KC, 3 * D], F32R)
        wproj = sb("wproj", [128, KC, D])
        wgnn = sb("wgnn", [128, KC, D])
        gamma_b = sb("gamma_b", [128, D])
        beta_b = sb("beta_b", [128, D])
        bias_rows = sb("bias_rows", [128, 2, D])
        bias_hi = sb("bias_hi", [128, 2, D], F32R)
        bias_lo = sb("bias_lo", [128, 2, D])
        bias_parts = sb("bias_parts", [128, 2, D], F32R)
        ones_f = sb("ones_f", [128, 128])
        ones_r = sb("ones_r", [128, 128], F32R)
        ident = sb("ident", [128, 128])
        adj_sb = sb("adj_sb", [128, N])
        adj_t = sb("adj_t", [128, N])
        block_add = sb("block_add", [128, N])
        minus_half, eps_col = sb("minus_half", [128, 1]), sb("eps_col", [128, 1])

        x_in = sb("x_in", [128, 2, D])
        xt_hi = sb("xt_hi", [128, KC, 2, N], F32R)
        xt_lo = sb("xt_lo", [128, KC, 2, N], F32R)
        q_t = sb("q_t", [128, KC, 2, N])
        k_t = sb("k_t", [128, KC, 2, N])
        k_diag = sb("k_diag", [128, KC, 2, HC, N])
        v_sb = sb("v_sb", [128, 2, D])
        x_plus_beta = sb("x_plus_beta", [128, B, D])
        probs = sb("probs", [128, 2, KC, HC, N])
        neg_max = sb("neg_max", [128, 2, H])
        row_sum = sb("row_sum", [128, 2, H])
        row_inv = sb("row_inv", [128, 2, H])
        probs_t = sb("probs_t", [128, 2, KC, HC, N])
        o_t = sb("o_t", [128, 2, KC, N])
        o_gamma = sb("o_gamma", [128, 2, D])
        o_plus_x = sb("o_plus_x", [128, 2, D])
        t_sb = sb("t_sb", [128, 2, D])
        x1 = sb("x1", [128, 2, D])
        y_t = sb("y_t", [128, 2, KC, N])
        u_sb = sb("u_sb", [128, 2, D])
        out_sb = sb("out_sb", [128, 2, D])
        o_raw, t_raw, u_raw = (sb(n, [128, 2, 6]) for n in ("o_raw", "t_raw", "u_raw"))
        o_mv, t_mv, u_mv = (sb(n, [128, 2, 2]) for n in ("o_mv", "t_mv", "u_mv"))
        o_ve, t_ve, u_ve = (sb(n, [128, 2, 1]) for n in ("o_ve", "t_ve", "u_ve"))
        o_rstd, t_rstd, u_rstd = (sb(n, [128, 2, 1]) for n in ("o_rstd", "t_rstd", "u_rstd"))

        scores = [bank("scores0"), bank("scores1")]
        trans = [bank("trans0"), bank("trans1")]
        kv_bank, qx_bank = bank("kv_bank"), bank("qx_bank")
        oy_bank, pw_bank = bank("oy_bank"), bank("pw_bank")

        x_loaded, k_diag_in = sem("x_loaded"), sem("k_diag_in")
        out_stored = [sem("out_stored0"), sem("out_stored1")]
        wqkv_in, adj_in, bias_in, beta_in = sem("wqkv_in"), sem("adj_in"), sem("bias_in"), sem("beta_in")
        gamma_in, wproj_in, wgnn_in = sem("gamma_in"), sem("wproj_in"), sem("wgnn_in")
        bias_zero, ident_zero, ident_made, kdiag_zero = (
            sem("bias_zero"), sem("ident_zero"), sem("ident_made"), sem("kdiag_zero"))
        half_made, hi_made, lo_made, bias_step = sem("half_made"), sem("hi_made"), sem("lo_made"), sem("bias_step")
        bias_made, ones_set, ones_made = sem("bias_made"), sem("ones_set"), sem("ones_made")
        adjt_done, adjt_made, mask_made = sem("adjt_done"), sem("adjt_made"), sem("mask_made")
        mask_turn = sem("mask_turn")
        xt_done, xt_hi_made, xt_lo_made = sem("xt_done"), sem("xt_hi_made"), sem("xt_lo_made")
        k_done, k_made, q_done, q_made = sem("k_done"), sem("k_made"), sem("q_done"), sem("q_made")
        v_done, v_made, x_added = sem("v_done"), sem("v_made"), sem("x_added")
        s_done = [sem("s_done0"), sem("s_done1")]
        masked = [sem("masked0"), sem("masked1")]
        exp_done = [sem("exp_done0"), sem("exp_done1")]
        inv_made = [sem("inv_made0"), sem("inv_made1")]
        normed = [sem("normed0"), sem("normed1")]
        pt_done = [sem("pt_done0"), sem("pt_done1")]
        pt_made = [sem("pt_made0"), sem("pt_made1")]
        pv_done, ot_made, proj_done = sem("pv_done"), sem("ot_made"), sem("proj_done")
        o_stats, o_moments, o_scaled, o_summed = sem("o_stats"), sem("o_moments"), sem("o_scaled"), sem("o_summed")
        o_eps, o_rstd_made = sem("o_eps"), sem("o_rstd_made")
        t_made, t_stats, t_moments, t_eps, t_rstd_made = (
            sem("t_made"), sem("t_stats"), sem("t_moments"), sem("t_eps"), sem("t_rstd_made"))
        x1_made, y_done, yt_made, w_done = sem("x1_made"), sem("y_done"), sem("yt_made"), sem("w_done")
        u_made, u_stats, u_moments, u_eps, u_rstd_made = (
            sem("u_made"), sem("u_stats"), sem("u_moments"), sem("u_eps"), sem("u_rstd_made"))
        out_made = sem("out_made")

        def pair_slots(eng, slot):
            FIRST, LAST = 3, PAIRS - 2
            for q in range(-1, FIRST):
                slot(q, 0, False)
                slot(q, 1, False)
            with eng.Fori(FIRST, LAST) as q:
                slot(q, 0, True)
                slot(q, 1, True)
            for q in range(LAST, PAIRS + 2):
                slot(q, 0, False)
                slot(q, 1, False)

        def real(b, steady):
            return steady or 0 <= b < B

        def real_pair(q, steady):
            return steady or 0 <= q < PAIRS

        block = ctx.enter_context(nc.Block())

        @block.sync
        def _(sp):
            sp.dma_start(x_in[:], x[0:2].rearrange("b n d -> n b d")).then_inc(x_loaded, 16)
            sp.dma_start(wqkv[:], w_qkv.rearrange("(c p) e -> p c e", p=128)).then_inc(wqkv_in, 16)
            sp.dma_start(adj_sb[:], adj).then_inc(adj_in, 16)
            sp.wait_ge(bias_zero, 1)
            for n, b in enumerate((b_proj, b_gnn)):
                sp.dma_start(bias_rows[0:2, n, :], b.partition_broadcast(2)).then_inc(bias_in, 16)
            sp.dma_start(beta_b[:], beta.partition_broadcast(128)).then_inc(beta_in, 16)
            sp.dma_start(gamma_b[:], gamma.partition_broadcast(128)).then_inc(gamma_in, 16)
            sp.dma_start(wproj[:], w_proj.rearrange("(c p) e -> p c e", p=128)).then_inc(wproj_in, 16)
            sp.dma_start(wgnn[:], w_gnn.rearrange("(c p) e -> p c e", p=128)).then_inc(wgnn_in, 16)

            def slot(q, par, steady):
                t = 2 * q + par
                if real(t - 4, steady):
                    sp.wait_ge(out_made, t - 3)
                    sp.dma_start(out[bass.ds(t - 4, 1)].rearrange("b n d -> n (b d)"),
                                 out_sb[:, par]).then_inc(out_stored[par], 16)
                if par == 0 and real_pair(q + 2, steady):
                    sp.wait_ge(xt_done, q + 2)
                    sp.wait_ge(x_added, q + 2)
                    sp.dma_start(x_in[:], x[bass.ds(2 * q + 4, 2)].rearrange("b n d -> n b d")).then_inc(x_loaded, 16)
                if par == 1 and real_pair(q + 1, steady):
                    sp.wait_ge(kdiag_zero, 1)
                    sp.wait_ge(k_made, q + 2)
                    if steady or q >= 0:
                        sp.wait_ge(s_done[1], t + 1)
                    for g in range(HC):
                        rows = slice(32 * g, 32 * g + 32)
                        sp.dma_start(k_diag[rows, :, :, g, :].rearrange("p c b m -> p (c b) m"),
                                     k_t[rows].rearrange("p c b m -> p (c b) m")).then_inc(k_diag_in, 16)

            pair_slots(sp, slot)
            for par in range(2):
                sp.wait_ge(out_stored[par], 16 * PAIRS)

        @block.gpsimd
        def _(pool):
            nc.gpsimd.memset(bias_rows[:], 0.0).then_inc(bias_zero, 1)
            nc.gpsimd.memset(ident[:], 0.0).then_inc(ident_zero, 1)
            pool.wait_ge(ident_zero, 1)
            nc.gpsimd.affine_select(out=ident[:], in_=ident[:], compare_op=ALU.not_equal, fill=1.0, base=0,
                                    pattern=[[-1, 128]], channel_multiplier=1).then_inc(ident_made, 1)
            nc.gpsimd.memset(k_diag[:], 0.0).then_inc(kdiag_zero, 1)
            nc.gpsimd.memset(minus_half[:], -0.5).then_inc(half_made, 1)
            nc.gpsimd.memset(eps_col[:], EPS).then_inc(half_made, 1)
            pool.wait_ge(half_made, 2)
            pool.wait_ge(beta_in, 16)

            def rstd(moments, count, par, mv, with_eps, eps_made, dest, made):
                pool.wait_ge(moments, count)
                nc.gpsimd.tensor_tensor(with_eps[:, par], mv[:, par, 1:2], eps_col[:], ALU.add).then_inc(eps_made, 1)
                pool.wait_ge(eps_made, count)
                nc.gpsimd.tensor_tensor(dest[:, par], with_eps[:, par], minus_half[:], ALU.pow).then_inc(made, 1)

            def normalise(t, par, c):
                pool.wait_ge(inv_made[c], t + 1)
                p = probs[:, par, c]
                nc.gpsimd.tensor_tensor(
                    p, p, row_inv[:, par, HC * c:HC * c + HC, None].to_broadcast([128, HC, N]),
                    ALU.mult).then_inc(normed[c], 1)

            def slot(q, par, steady):
                t = 2 * q + par
                if real(t - 2, steady):
                    rstd(o_moments, t - 1, par, o_mv, o_ve, o_eps, o_rstd, o_rstd_made)
                if par == 0 and real_pair(q + 1, steady):
                    pool.wait_ge(x_loaded, 16 * (q + 2))
                    nc.gpsimd.tensor_tensor(
                        x_plus_beta[:, bass.ds(2 * q + 2, 2)], x_in[:],
                        beta_b[:, None, :].to_broadcast([128, 2, D]), ALU.add).then_inc(x_added, 1)
                if real(t - 2, steady):
                    rstd(t_moments, t - 1, par, t_mv, t_ve, t_eps, t_rstd, t_rstd_made)
                if real(t, steady):
                    normalise(t, par, 0)
                if real(t - 3, steady):
                    rstd(u_moments, t - 2, 1 - par, u_mv, u_ve, u_eps, u_rstd, u_rstd_made)
                if real(t, steady):
                    normalise(t, par, 1)

            pair_slots(pool, slot)

        @block.scalar
        def _(act):
            act.wait_ge(wqkv_in, 16)
            nc.scalar.activation(wqkv_hi[:], wqkv[:], ACT.Copy).then_inc(hi_made, 1)
            act.wait_ge(adjt_done, 1)
            nc.scalar.activation(adj_t[:], trans[0][:, 0:N], ACT.Copy).then_inc(adjt_made, 1)

            def slot(q, par, steady):
                t = 2 * q + par
                if real(t - 3, steady):
                    act.wait_ge(y_done, t - 2)
                    nc.scalar.activation(y_t[:, 1 - par], oy_bank[:, 0:D].rearrange("p (c n) -> p c n", c=KC),
                                         ACT.Copy).then_inc(yt_made, 1)
                if real(t - 1, steady):
                    for c in range(KC):
                        act.wait_ge(pt_done[c], t)
                        nc.scalar.activation(probs_t[:, 1 - par, c], trans[c][:].rearrange("p (j n) -> p j n", j=HC),
                                             ACT.Copy).then_inc(pt_made[c], 1)
                for c in range(KC):
                    if real(t, steady):
                        act.wait_ge(masked[c], t + 1)
                        if steady or t >= 2:
                            act.wait_ge(pt_done[c], t - 1)
                        for j in range(HC):
                            h = HC * c + j
                            last = nc.scalar.activation(
                                probs[:, par, c, j], scores[c][:, j * N:j * N + N], ACT.Exp,
                                bias=neg_max[:, par, h:h + 1], scale=-1.0, accum_out=row_sum[:, par, h:h + 1])
                        last.then_inc(exp_done[c], 1)
                    if c == 0 and par == 1 and real_pair(q + 1, steady):
                        act.wait_ge(k_done, q + 2)
                        if steady or q >= 0:
                            act.wait_ge(k_diag_in, 16 * HC * (q + 1))
                        nc.scalar.activation(k_t[:], kv_bank[:].rearrange("p (c b m) -> p c b m", c=KC, b=2),
                                             ACT.Copy).then_inc(k_made, 1)
                if real(t - 1, steady):
                    act.wait_ge(pv_done, t)
                    nc.scalar.activation(o_t[:, 1 - par], oy_bank[:, 0:D].rearrange("p (c n) -> p c n", c=KC),
                                         ACT.Copy).then_inc(ot_made, 1)
                if par == 1 and real_pair(q + 1, steady):
                    act.wait_ge(q_done, q + 2)
                    nc.scalar.activation(q_t[:], qx_bank[:].rearrange("p (c b n) -> p c b n", c=KC, b=2),
                                         ACT.Copy, scale=-SCALE).then_inc(q_made, 1)
                if par == 0 and real_pair(q, steady):
                    act.wait_ge(v_done, q + 1)
                    nc.scalar.activation(v_sb[:], kv_bank[:].rearrange("p (b d) -> p b d", b=2),
                                         ACT.Copy).then_inc(v_made, 1)
                if par == 0 and real_pair(q + 1, steady):
                    act.wait_ge(xt_done, q + 2)
                    nc.scalar.activation(xt_hi[:], qx_bank[:].rearrange("p (c b n) -> p c b n", c=KC, b=2),
                                         ACT.Copy).then_inc(xt_hi_made, 1)

            pair_slots(act, slot)

        @block.vector
        def _(dve):
            nc.vector.memset(ones_f[:], 1.0).then_inc(ones_set, 1)
            dve.wait_ge(ones_set, 1)
            nc.vector.tensor_copy(ones_r[:], ones_f[:]).then_inc(ones_made, 1)
            dve.wait_ge(hi_made, 1)
            nc.vector.tensor_tensor(wqkv_lo[:], wqkv[:], wqkv_hi[:].bitcast(F32), ALU.subtract).then_inc(lo_made, 1)
            dve.wait_ge(bias_in, 32)
            nc.vector.tensor_copy(bias_hi[:], bias_rows[:]).then_inc(bias_step, 1)
            dve.wait_ge(bias_step, 1)
            nc.vector.tensor_tensor(bias_lo[:], bias_rows[:], bias_hi[:].bitcast(F32), ALU.subtract).then_inc(bias_step, 1)
            dve.wait_ge(bias_step, 2)
            dve.wait_ge(ident_made, 1)
            nc.vector.tensor_scalar(bias_lo[:], bias_lo[:], ident[:, 1:2], None, ALU.mult).then_inc(bias_step, 1)
            dve.wait_ge(bias_step, 3)
            for n in range(2):
                last = nc.vector.scalar_tensor_tensor(bias_parts[:, n], bias_hi[:, n].bitcast(F32), ident[:, 0:1],
                                                      bias_lo[:, n], ALU.mult, ALU.add)
            last.then_inc(bias_made, 1)
            dve.wait_ge(adj_in, 16)
            nc.vector.tensor_scalar(block_add[:], adj_sb[:], 0.0, BLOCKED, ALU.is_equal, ALU.mult).then_inc(mask_made, 1)
            dve.wait_ge(gamma_in, 16)

            def slot(q, par, steady):
                t = 2 * q + par
                if real(t - 4, steady):
                    dve.wait_ge(u_rstd_made, t - 3)
                    if steady or t - 6 >= 0:
                        dve.wait_ge(out_stored[par], 16 * (q - 2))
                    nc.vector.tensor_scalar(out_sb[:, par], u_sb[:, par], u_mv[:, par, 0:1], u_rstd[:, par],
                                            ALU.subtract, ALU.mult).then_inc(out_made, 1)
                if real(t - 2, steady):
                    o = pw_bank[:, 0:D]
                    dve.wait_ge(proj_done, t - 1)
                    nc.vector.bn_stats(o_raw[:, par], o).then_inc(o_stats, 1)
                    dve.wait_ge(mask_made, 1)
                    dve.wait_ge(o_stats, t - 1)
                    nc.vector.bn_aggr(o_mv[:, par], o_raw[:, par]).then_inc(o_moments, 1)
                    dve.wait_ge(x_added, q)
                    nc.vector.tensor_tensor(o_plus_x[:, par], o, x_plus_beta[:, bass.ds(t - 2, 1)].rearrange(
                        "p b d -> p (b d)"), ALU.add).then_inc(o_summed, 1)
                    dve.wait_ge(o_moments, t - 1)
                    nc.vector.scalar_tensor_tensor(o_gamma[:, par], o, o_mv[:, par, 0:1], gamma_b[:],
                                                   ALU.subtract, ALU.mult).then_inc(o_scaled, 1)
                if real(t, steady):
                    for c in range(KC):
                        dve.wait_ge(s_done[c], t + 1)
                        dve.sem_inc(mask_turn, 1)
                        for j in range(HC):
                            s, h = scores[c][:, j * N:j * N + N], HC * c + j
                            last = nc.vector.tensor_tensor_reduce(
                                out=s, in0=s, in1=block_add[:], scale=1.0, scalar=HUGE, op0=ALU.add, op1=ALU.min,
                                accum_out=neg_max[:, par, h:h + 1])
                        last.then_inc(masked[c], 1)
                if real(t - 2, steady):
                    dve.wait_ge(o_rstd_made, t - 1)
                    dve.wait_ge(o_scaled, t - 1)
                    dve.wait_ge(o_summed, t - 1)
                    nc.vector.scalar_tensor_tensor(t_sb[:, par], o_gamma[:, par], o_rstd[:, par], o_plus_x[:, par],
                                                   ALU.mult, ALU.add).then_inc(t_made, 1)
                    dve.wait_ge(t_made, t - 1)
                    nc.vector.bn_stats(t_raw[:, par], t_sb[:, par]).then_inc(t_stats, 1)
                    dve.wait_ge(mask_made, 1)
                    dve.wait_ge(t_stats, t - 1)
                    nc.vector.bn_aggr(t_mv[:, par], t_raw[:, par]).then_inc(t_moments, 1)
                if real(t, steady):
                    dve.wait_ge(exp_done[0], t + 1)
                    nc.vector.reciprocal(row_inv[:, par, 0:HC], row_sum[:, par, 0:HC]).then_inc(inv_made[0], 1)
                if real(t - 3, steady):
                    dve.wait_ge(w_done, t - 2)
                    dve.wait_ge(x1_made, t - 2)
                    nc.vector.tensor_tensor(u_sb[:, 1 - par], pw_bank[:, 0:D], x1[:, 1 - par], ALU.add).then_inc(u_made, 1)
                    dve.wait_ge(u_made, t - 2)
                    nc.vector.bn_stats(u_raw[:, 1 - par], u_sb[:, 1 - par]).then_inc(u_stats, 1)
                    dve.wait_ge(mask_made, 1)
                    dve.wait_ge(u_stats, t - 2)
                    nc.vector.bn_aggr(u_mv[:, 1 - par], u_raw[:, 1 - par]).then_inc(u_moments, 1)
                if real(t - 2, steady):
                    dve.wait_ge(t_rstd_made, t - 1)
                    nc.vector.tensor_scalar(x1[:, par], t_sb[:, par], t_mv[:, par, 0:1], t_rstd[:, par],
                                            ALU.subtract, ALU.mult).then_inc(x1_made, 1)
                if real(t, steady):
                    dve.wait_ge(exp_done[1], t + 1)
                    nc.vector.reciprocal(row_inv[:, par, HC:H], row_sum[:, par, HC:H]).then_inc(inv_made[1], 1)
                if par == 0 and real_pair(q + 1, steady):
                    dve.wait_ge(xt_hi_made, q + 2)
                    nc.vector.tensor_tensor(xt_lo[:], qx_bank[:].rearrange("p (c b n) -> p c b n", c=KC, b=2),
                                            xt_hi[:].bitcast(F32), ALU.subtract).then_inc(xt_lo_made, 1)

            pair_slots(dve, slot)

        @block.tensor
        def _(pe):
            pe.wait_ge(ident_made, 1)
            pe.wait_ge(adj_in, 16)
            nc.tensor.transpose(trans[0][:, 0:N], adj_sb[:], ident[:]).then_inc(adjt_done, 1)

            def product(dest, parts_l, parts_r):
                terms = [(i, j, c) for i, j in ((0, 0), (0, 1), (1, 0)) for c in range(KC)]
                for n, (i, j, c) in enumerate(terms):
                    last = nc.tensor.matmul(dest, parts_l[i](c), parts_r[j](c), start=n == 0, stop=n == len(terms) - 1)
                return last

            def q_or_k(dest, first_col):
                for m in range(KC):
                    cols = slice(first_col + 128 * m, first_col + 128 * m + 128)
                    last = product(dest[:, 2 * N * m:2 * N * m + 2 * N],
                                   [lambda c, w=w, cols=cols: w[:, c, cols] for w in (wqkv_hi, wqkv_lo)],
                                   [lambda c, xt=xt: xt[:, c].rearrange("p b n -> p (b n)") for xt in (xt_hi, xt_lo)])
                return last

            def slot(q, par, steady):
                t = 2 * q + par
                if real(t, steady):
                    pe.wait_ge(k_diag_in, 16 * HC * (q + 1))
                    pe.wait_ge(q_made, q + 1)
                    for c in range(KC):
                        if steady or t >= 1:
                            pe.wait_ge(exp_done[c], t)
                        nc.tensor.matmul(scores[c][:], q_t[:, c, par], k_diag[:, c, par].rearrange("p j m -> p (j m)"),
                                         start=True, stop=True).then_inc(s_done[c], 1)
                if real(t - 3, steady):
                    pe.wait_ge(x1_made, t - 2)
                    if steady or real(t - 2, False):
                        pe.wait_ge(ot_made, t - 1)
                    for c in range(KC):
                        last = nc.tensor.matmul(oy_bank[:, c * N:c * N + N], x1[:, 1 - par, 128 * c:128 * c + 128],
                                                adj_t[:], start=True, stop=True)
                    last.then_inc(y_done, 1)
                if real(t - 1, steady):
                    for c in range(KC):
                        pe.wait_ge(normed[c], t)
                        if steady or t >= 2:
                            pe.wait_ge(pt_made[c], t - 1)
                        for j in range(HC):
                            last = nc.tensor.transpose(trans[c][:, j * N:j * N + N], probs[:, 1 - par, c, j], ident[:])
                        last.then_inc(pt_done[c], 1)
                if par == 1 and real_pair(q + 1, steady):
                    pe.wait_ge(xt_hi_made, q + 2)
                    pe.wait_ge(xt_lo_made, q + 2)
                    if steady or q >= 0:
                        pe.wait_ge(v_made, q + 1)
                    q_or_k(kv_bank, D).then_inc(k_done, 1)
                if real(t - 3, steady):
                    pe.wait_ge(yt_made, t - 2)
                    if steady or real(t - 2, False):
                        pe.wait_ge(o_scaled, t - 1)
                    nc.tensor.matmul(pw_bank[:, 0:D], ones_r[:], bias_parts[:, 1], start=True, stop=False)
                    for c in range(KC):
                        last = nc.tensor.matmul(pw_bank[:, 0:D], y_t[:, 1 - par, c], wgnn[:, c],
                                                start=False, stop=c == KC - 1)
                    last.then_inc(w_done, 1)
                if real(t - 1, steady):
                    pe.wait_ge(v_made, q + par)
                    if steady or real(t - 3, False):
                        pe.wait_ge(yt_made, t - 2)
                    for c in range(KC):
                        pe.wait_ge(pt_made[c], t)
                        for j in range(HC):
                            first = 32 * (HC * c + j)
                            last = nc.tensor.matmul(oy_bank[32 * j:32 * j + 32, c * N:c * N + N],
                                                    v_sb[:, 1 - par, first:first + 32], probs_t[:, 1 - par, c, j],
                                                    start=True, stop=True)
                    last.then_inc(pv_done, 1)
                if par == 1 and real_pair(q + 1, steady):
                    q_or_k(qx_bank, 0).then_inc(q_done, 1)
                if par == 0 and real_pair(q, steady):
                    pe.wait_ge(k_made, q + 1)
                    for b in range(2):
                        last = product(kv_bank[:, D * b:D * b + D],
                                       [lambda c, xt=xt, b=b: xt[:, c, b] for xt in (xt_hi, xt_lo)],
                                       [lambda c, w=w: w[:, c, 2 * D:3 * D] for w in (wqkv_hi, wqkv_lo)])
                    last.then_inc(v_done, 1)
                if real(t - 1, steady):
                    pe.wait_ge(ot_made, t)
                    if steady or real(t - 3, False):
                        pe.wait_ge(u_made, t - 2)
                    nc.tensor.matmul(pw_bank[:, 0:D], ones_r[:], bias_parts[:, 0], start=True, stop=False)
                    for c in range(KC):
                        last = nc.tensor.matmul(pw_bank[:, 0:D], o_t[:, 1 - par, c], wproj[:, c],
                                                start=False, stop=c == KC - 1)
                    last.then_inc(proj_done, 1)
                if par == 0 and real_pair(q + 1, steady):
                    pe.wait_ge(x_loaded, 16 * (q + 2))
                    if steady or q >= 0:
                        pe.wait_ge(q_made, q + 1)
                    for c in range(KC):
                        for b in range(2):
                            at = (2 * c + b) * N
                            last = nc.tensor.transpose(qx_bank[:, at:at + N], x_in[:, b, 128 * c:128 * c + 128], ident[:])
                    last.then_inc(xt_done, 1)

            pe.wait_ge(ones_made, 1)
            pe.wait_ge(bias_made, 1)
            pe.wait_ge(lo_made, 1)
            pe.wait_ge(adjt_made, 1)
            pe.wait_ge(wproj_in, 16)
            pe.wait_ge(wgnn_in, 16)
            pair_slots(pe, slot)


INPUTS = ["x", "adj", "L0_gnn_w_qkv", "L0_gnn_w_proj", "L0_gnn_b_proj", "L0_gnn_ln_gamma", "L0_gnn_ln_beta",
          "L1_gnn_weight", "L1_gnn_bias"]


def kernel(**inputs):
    import numpy as np
    import concourse.bacc as bacc
    from concourse.bass_utils import run_bass_kernel_spmd

    nc = bacc.Bacc("TRN2", target_bir_lowering=False, num_devices=1)
    arrays, args = {}, []
    for name in INPUTS:
        a = np.ascontiguousarray(inputs[name])
        arrays[f"in_{name}"] = a
        args.append(nc.dram_tensor(f"in_{name}", a.shape, mybir.dt.from_np(a.dtype), kind="ExternalInput").ap())
    args.append(nc.dram_tensor("result", inputs["x"].shape, F32, kind="ExternalOutput").ap())
    gnn_block_kernel(nc, *args)
    return run_bass_kernel_spmd(nc, [arrays], core_ids=[0]).results[0]["result"]
```

```python
import concourse.bass as bass
from concourse import mybir
from contextlib import ExitStack

F32 = mybir.dt.float32
F32R = mybir.dt.float32r
ALU = mybir.AluOpType
ACT = mybir.ActivationFunctionType


def gnn_block_kernel(nc, x, adj, w_qkv, w_proj, b_proj, gamma, beta, w_gnn, b_gnn, out):
    B, N, D = x.shape
    HD = 32
    H = D // HD
    KC = D // 128
    HC = H // KC
    PAIRS = B // 2
    SCALE = float(HD) ** -0.5
    EPS = 1e-5
    BLOCKED = -1e30
    HUGE = 3e38

    ctx = ExitStack()
    with ctx:
        def sb(name, shape, dt=F32):
            return ctx.enter_context(nc.sbuf_tensor(name, shape, dt))

        def bank(name):
            return ctx.enter_context(nc.psum_tensor(name, [128, 512], F32))

        def sem(name):
            return ctx.enter_context(nc.semaphore(name))

        wqkv = sb("wqkv", [128, KC, 3 * D])
        wqkv_hi = sb("wqkv_hi", [128, KC, 3 * D], F32R)
        wqkv_lo = sb("wqkv_lo", [128, KC, 3 * D], F32R)
        wproj, wgnn = sb("wproj", [128, KC, D]), sb("wgnn", [128, KC, D])
        wproj_hi, wproj_lo = sb("wproj_hi", [128, KC, D], F32R), sb("wproj_lo", [128, KC, D], F32R)
        wgnn_hi, wgnn_lo = sb("wgnn_hi", [128, KC, D], F32R), sb("wgnn_lo", [128, KC, D], F32R)
        gamma_b = sb("gamma_b", [128, D])
        beta_b = sb("beta_b", [128, D])
        bias_rows = sb("bias_rows", [128, 2, D])
        bias_hi = sb("bias_hi", [128, 2, D], F32R)
        bias_lo = sb("bias_lo", [128, 2, D])
        bias_parts = sb("bias_parts", [128, 2, D], F32R)
        ones_f = sb("ones_f", [128, 128])
        ones_r = sb("ones_r", [128, 128], F32R)
        ident = sb("ident", [128, 128])
        adj_sb = sb("adj_sb", [128, N])
        adj_t = sb("adj_t", [128, N])
        block_add = sb("block_add", [128, N])
        minus_half, eps_col = sb("minus_half", [128, 1]), sb("eps_col", [128, 1])

        x_in = sb("x_in", [128, 2, D])
        xt_hi = sb("xt_hi", [128, 2, KC, 2, N], F32R)
        xt_lo = sb("xt_lo", [128, 2, KC, 2, N], F32R)
        q_t = sb("q_t", [128, 2, 2, KC, 2, N], F32R)
        k_t = sb("k_t", [128, 2, 2, KC, 2, N], F32R)
        k_diag = sb("k_diag", [128, 2, 2, KC, 2, HC, N], F32R)
        v_sb = sb("v_sb", [128, 2, 2, D])
        x_plus_beta = sb("x_plus_beta", [128, B, D])
        probs = sb("probs", [128, 2, KC, HC, N])
        neg_max = sb("neg_max", [128, 2, H])
        row_sum = sb("row_sum", [128, 2, H])
        row_inv = sb("row_inv", [128, 2, H])
        probs_t = sb("probs_t", [128, 2, KC, HC, N])
        o_t_hi, o_t_lo = sb("o_t_hi", [128, 2, KC, N], F32R), sb("o_t_lo", [128, 2, KC, N], F32R)
        o_gamma = sb("o_gamma", [128, 2, D])
        o_plus_x = sb("o_plus_x", [128, 2, D])
        t_sb = sb("t_sb", [128, 2, D])
        x1 = sb("x1", [128, 2, D])
        y_t_hi, y_t_lo = sb("y_t_hi", [128, 2, KC, N], F32R), sb("y_t_lo", [128, 2, KC, N], F32R)
        u_sb = sb("u_sb", [128, 2, D])
        out_sb = sb("out_sb", [128, 2, D])
        o_raw, t_raw, u_raw = (sb(n, [128, 2, 6]) for n in ("o_raw", "t_raw", "u_raw"))
        o_mv, t_mv, u_mv = (sb(n, [128, 2, 2]) for n in ("o_mv", "t_mv", "u_mv"))
        o_ve, t_ve, u_ve = (sb(n, [128, 2, 1]) for n in ("o_ve", "t_ve", "u_ve"))
        o_rstd, t_rstd, u_rstd = (sb(n, [128, 2, 1]) for n in ("o_rstd", "t_rstd", "u_rstd"))

        scores = [bank("scores0"), bank("scores1")]
        trans = [bank("trans0"), bank("trans1")]
        kv_bank, qx_bank = bank("kv_bank"), bank("qx_bank")
        oy_bank, pw_bank = bank("oy_bank"), bank("pw_bank")

        x_loaded, k_diag_in = sem("x_loaded"), sem("k_diag_in")
        out_stored = [sem("out_stored0"), sem("out_stored1")]
        wqkv_in, adj_in, bias_in, beta_in = sem("wqkv_in"), sem("adj_in"), sem("bias_in"), sem("beta_in")
        gamma_in, wproj_in, wgnn_in = sem("gamma_in"), sem("wproj_in"), sem("wgnn_in")
        bias_zero, ident_zero, ident_made, kdiag_zero = (
            sem("bias_zero"), sem("ident_zero"), sem("ident_made"), sem("kdiag_zero"))
        half_made, hi_made, lo_made, bias_step = sem("half_made"), sem("hi_made"), sem("lo_made"), sem("bias_step")
        bias_made, ones_set, ones_made = sem("bias_made"), sem("ones_set"), sem("ones_made")
        adjt_done, adjt_made, mask_made = sem("adjt_done"), sem("adjt_made"), sem("mask_made")
        mask_turn = sem("mask_turn")
        xt_done, xt_hi_made, xt_lo_made = sem("xt_done"), sem("xt_hi_made"), sem("xt_lo_made")
        k_done, k_hi_made, k_lo_made = sem("k_done"), sem("k_hi_made"), sem("k_lo_made")
        q_done, q_hi_made, q_lo_made = sem("q_done"), sem("q_hi_made"), sem("q_lo_made")
        v_done, v_made, x_added = sem("v_done"), sem("v_made"), sem("x_added")
        s_done = [sem("s_done0"), sem("s_done1")]
        masked = [sem("masked0"), sem("masked1")]
        exp_done = [sem("exp_done0"), sem("exp_done1")]
        inv_made = [sem("inv_made0"), sem("inv_made1")]
        normed = [sem("normed0"), sem("normed1")]
        pt_done = [sem("pt_done0"), sem("pt_done1")]
        pt_made = [sem("pt_made0"), sem("pt_made1")]
        pv_done, ot_hi_made, ot_lo_made, proj_done = (
            sem("pv_done"), sem("ot_hi_made"), sem("ot_lo_made"), sem("proj_done"))
        o_stats, o_moments, o_scaled, o_summed = sem("o_stats"), sem("o_moments"), sem("o_scaled"), sem("o_summed")
        o_eps, o_rstd_made = sem("o_eps"), sem("o_rstd_made")
        t_made, t_stats, t_moments, t_eps, t_rstd_made = (
            sem("t_made"), sem("t_stats"), sem("t_moments"), sem("t_eps"), sem("t_rstd_made"))
        x1_made, y_done, yt_hi_made, yt_lo_made, w_done = (
            sem("x1_made"), sem("y_done"), sem("yt_hi_made"), sem("yt_lo_made"), sem("w_done"))
        u_made, u_stats, u_moments, u_eps, u_rstd_made = (
            sem("u_made"), sem("u_stats"), sem("u_moments"), sem("u_eps"), sem("u_rstd_made"))
        out_made = sem("out_made")

        def pair_slots(eng, slot):
            FIRST, LAST = 2, PAIRS // 2 - 2

            def pair(q, buf, steady):
                slot(q, 0, buf, steady)
                slot(q, 1, buf, steady)

            for q in range(-2, 2 * FIRST):
                pair(q, q % 2, False)
            with eng.Fori(FIRST, LAST) as r:
                pair(2 * r, 0, True)
                pair(2 * r + 1, 1, True)
            for q in range(2 * LAST, PAIRS + 2):
                pair(q, q % 2, False)

        def real(b, steady):
            return steady or 0 <= b < B

        def real_pair(q, steady):
            return steady or 0 <= q < PAIRS

        block = ctx.enter_context(nc.Block())

        @block.sync
        def _(sp):
            sp.dma_start(x_in[:], x[0:2].rearrange("b n d -> n b d")).then_inc(x_loaded, 16)
            sp.dma_start(wqkv[:], w_qkv.rearrange("(c p) e -> p c e", p=128)).then_inc(wqkv_in, 16)
            sp.dma_start(adj_sb[:], adj).then_inc(adj_in, 16)
            sp.wait_ge(bias_zero, 1)
            for n, b in enumerate((b_proj, b_gnn)):
                sp.dma_start(bias_rows[0:2, n, :], b.partition_broadcast(2)).then_inc(bias_in, 16)
            sp.dma_start(beta_b[:], beta.partition_broadcast(128)).then_inc(beta_in, 16)
            sp.dma_start(gamma_b[:], gamma.partition_broadcast(128)).then_inc(gamma_in, 16)
            sp.dma_start(wproj[:], w_proj.rearrange("(c p) e -> p c e", p=128)).then_inc(wproj_in, 16)
            sp.dma_start(wgnn[:], w_gnn.rearrange("(c p) e -> p c e", p=128)).then_inc(wgnn_in, 16)

            def slot(q, par, buf, steady):
                t = 2 * q + par
                if real(t - 4, steady):
                    sp.wait_ge(out_made, t - 3)
                    sp.dma_start(out[bass.ds(t - 4, 1)].rearrange("b n d -> n (b d)"),
                                 out_sb[:, par]).then_inc(out_stored[par], 16)
                if par == 0 and real_pair(q + 1, steady):
                    sp.wait_ge(kdiag_zero, 1)
                    sp.wait_ge(k_hi_made, q + 2)
                    sp.wait_ge(k_lo_made, q + 2)
                    if steady or q >= 1:
                        sp.wait_ge(s_done[1], t)
                    for g in range(HC):
                        rows = slice(32 * g, 32 * g + 32)
                        sp.dma_start(k_diag[rows, 1 - buf, :, :, :, g, :].bitcast(F32).rearrange("p i c b m -> p (i c b) m"),
                                     k_t[rows, 1 - buf].bitcast(F32).rearrange("p i c b m -> p (i c b) m")
                                     ).then_inc(k_diag_in, 16)
                if par == 1 and real_pair(q + 3, steady):
                    sp.wait_ge(xt_done, q + 3)
                    sp.wait_ge(x_added, q + 3)
                    sp.dma_start(x_in[:], x[bass.ds(2 * q + 6, 2)].rearrange("b n d -> n b d")).then_inc(x_loaded, 16)

            pair_slots(sp, slot)
            for par in range(2):
                sp.wait_ge(out_stored[par], 16 * PAIRS)

        @block.gpsimd
        def _(pool):
            nc.gpsimd.memset(bias_rows[:], 0.0).then_inc(bias_zero, 1)
            nc.gpsimd.memset(ident[:], 0.0).then_inc(ident_zero, 1)
            pool.wait_ge(ident_zero, 1)
            nc.gpsimd.affine_select(out=ident[:], in_=ident[:], compare_op=ALU.not_equal, fill=1.0, base=0,
                                    pattern=[[-1, 128]], channel_multiplier=1).then_inc(ident_made, 1)
            nc.gpsimd.memset(k_diag[:].bitcast(F32), 0.0).then_inc(kdiag_zero, 1)
            nc.gpsimd.memset(minus_half[:], -0.5).then_inc(half_made, 1)
            nc.gpsimd.memset(eps_col[:], EPS).then_inc(half_made, 1)
            pool.wait_ge(half_made, 2)
            pool.wait_ge(beta_in, 16)

            def rstd(moments, count, par, mv, with_eps, eps_made, dest, made):
                pool.wait_ge(moments, count)
                nc.gpsimd.tensor_tensor(with_eps[:, par], mv[:, par, 1:2], eps_col[:], ALU.add).then_inc(eps_made, 1)
                pool.wait_ge(eps_made, count)
                nc.gpsimd.tensor_tensor(dest[:, par], with_eps[:, par], minus_half[:], ALU.pow).then_inc(made, 1)

            def normalise(t, par, c):
                pool.wait_ge(inv_made[c], t + 1)
                p = probs[:, par, c]
                nc.gpsimd.tensor_tensor(
                    p, p, row_inv[:, par, HC * c:HC * c + HC, None].to_broadcast([128, HC, N]),
                    ALU.mult).then_inc(normed[c], 1)

            def slot(q, par, buf, steady):
                t = 2 * q + par
                if real(t - 2, steady):
                    rstd(o_moments, t - 1, par, o_mv, o_ve, o_eps, o_rstd, o_rstd_made)
                if real(t, steady):
                    normalise(t, par, 0)
                if par == 1 and real_pair(q + 2, steady):
                    pool.wait_ge(x_loaded, 16 * (q + 3))
                    nc.gpsimd.tensor_tensor(
                        x_plus_beta[:, bass.ds(2 * q + 4, 2)], x_in[:],
                        beta_b[:, None, :].to_broadcast([128, 2, D]), ALU.add).then_inc(x_added, 1)
                if real(t - 2, steady):
                    rstd(t_moments, t - 1, par, t_mv, t_ve, t_eps, t_rstd, t_rstd_made)
                if real(t, steady):
                    normalise(t, par, 1)
                if real(t - 3, steady):
                    rstd(u_moments, t - 2, 1 - par, u_mv, u_ve, u_eps, u_rstd, u_rstd_made)

            pair_slots(pool, slot)

        @block.scalar
        def _(act):
            act.wait_ge(wqkv_in, 16)
            nc.scalar.activation(wqkv_hi[:], wqkv[:], ACT.Copy).then_inc(hi_made, 1)
            act.wait_ge(wproj_in, 16)
            nc.scalar.activation(wproj_hi[:], wproj[:], ACT.Copy).then_inc(hi_made, 1)
            act.wait_ge(wgnn_in, 16)
            nc.scalar.activation(wgnn_hi[:], wgnn[:], ACT.Copy).then_inc(hi_made, 1)
            act.wait_ge(adjt_done, 1)
            nc.scalar.activation(adj_t[:], trans[0][:, 0:N], ACT.Copy).then_inc(adjt_made, 1)

            def slot(q, par, buf, steady):
                t = 2 * q + par

                def exps(c, heads):
                    if real(t, steady):
                        if heads[0] == 0:
                            act.wait_ge(masked[c], t + 1)
                            if steady or t >= 2:
                                act.wait_ge(pt_done[c], t - 1)
                        for j in heads:
                            h = HC * c + j
                            last = nc.scalar.activation(
                                probs[:, par, c, j], scores[c][:, j * N:j * N + N], ACT.Exp,
                                bias=neg_max[:, par, h:h + 1], scale=-1.0, accum_out=row_sum[:, par, h:h + 1])
                        if heads[-1] == HC - 1:
                            last.then_inc(exp_done[c], 1)

                exps(0, range(HC))
                if par == 0 and real_pair(q + 1, steady):
                    act.wait_ge(k_done, q + 2)
                    if steady or q >= 1:
                        act.wait_ge(k_diag_in, 16 * HC * q)
                    nc.scalar.activation(k_t[:, 1 - buf, 0], kv_bank[:].rearrange("p (c b m) -> p c b m", c=KC, b=2),
                                         ACT.Copy).then_inc(k_hi_made, 1)
                if par == 1 and real_pair(q + 1, steady):
                    act.wait_ge(v_done, q + 2)
                    nc.scalar.activation(v_sb[:, 1 - buf], kv_bank[:].rearrange("p (b d) -> p b d", b=2),
                                         ACT.Copy).then_inc(v_made, 1)
                if real(t - 3, steady):
                    act.wait_ge(y_done, t - 2)
                    nc.scalar.activation(y_t_hi[:, 1 - par], oy_bank[:, 0:D].rearrange("p (c n) -> p c n", c=KC),
                                         ACT.Copy).then_inc(yt_hi_made, 1)
                if real(t - 1, steady):
                    for c in range(KC):
                        act.wait_ge(pt_done[c], t)
                        nc.scalar.activation(probs_t[:, 1 - par, c], trans[c][:].rearrange("p (j n) -> p j n", j=HC),
                                             ACT.Copy).then_inc(pt_made[c], 1)
                exps(1, range(HC // 2))
                if real(t - 1, steady):
                    act.wait_ge(pv_done, t)
                    nc.scalar.activation(o_t_hi[:, 1 - par], oy_bank[:, 0:D].rearrange("p (c n) -> p c n", c=KC),
                                         ACT.Copy).then_inc(ot_hi_made, 1)
                exps(1, range(HC // 2, HC))
                if par == 0 and real_pair(q + 1, steady):
                    act.wait_ge(q_done, q + 2)
                    nc.scalar.activation(q_t[:, 1 - buf, 0], qx_bank[:].rearrange("p (c b n) -> p c b n", c=KC, b=2),
                                         ACT.Copy).then_inc(q_hi_made, 1)
                if par == 1 and real_pair(q + 2, steady):
                    act.wait_ge(xt_done, q + 3)
                    nc.scalar.activation(xt_hi[:, buf], qx_bank[:].rearrange("p (c b n) -> p c b n", c=KC, b=2),
                                         ACT.Copy).then_inc(xt_hi_made, 1)

            pair_slots(act, slot)

        @block.vector
        def _(dve):
            nc.vector.memset(ones_f[:], 1.0).then_inc(ones_set, 1)
            dve.wait_ge(ones_set, 1)
            nc.vector.tensor_copy(ones_r[:], ones_f[:]).then_inc(ones_made, 1)
            for n, (w, hi, lo) in enumerate(((wqkv, wqkv_hi, wqkv_lo), (wproj, wproj_hi, wproj_lo),
                                             (wgnn, wgnn_hi, wgnn_lo))):
                dve.wait_ge(hi_made, n + 1)
                nc.vector.tensor_tensor(lo[:], w[:], hi[:].bitcast(F32), ALU.subtract).then_inc(lo_made, 1)
            dve.wait_ge(bias_in, 32)
            nc.vector.tensor_copy(bias_hi[:], bias_rows[:]).then_inc(bias_step, 1)
            dve.wait_ge(bias_step, 1)
            nc.vector.tensor_tensor(bias_lo[:], bias_rows[:], bias_hi[:].bitcast(F32), ALU.subtract).then_inc(bias_step, 1)
            dve.wait_ge(bias_step, 2)
            dve.wait_ge(ident_made, 1)
            nc.vector.tensor_scalar(bias_lo[:], bias_lo[:], ident[:, 1:2], None, ALU.mult).then_inc(bias_step, 1)
            dve.wait_ge(bias_step, 3)
            for n in range(2):
                last = nc.vector.scalar_tensor_tensor(bias_parts[:, n], bias_hi[:, n].bitcast(F32), ident[:, 0:1],
                                                      bias_lo[:, n], ALU.mult, ALU.add)
            last.then_inc(bias_made, 1)
            dve.wait_ge(adj_in, 16)
            nc.vector.tensor_scalar(block_add[:], adj_sb[:], 0.0, BLOCKED, ALU.is_equal, ALU.mult).then_inc(mask_made, 1)
            dve.wait_ge(gamma_in, 16)

            def low_part(made, count, low, full, high, low_made):
                dve.wait_ge(made, count)
                nc.vector.tensor_tensor(low, full, high.bitcast(F32), ALU.subtract).then_inc(low_made, 1)

            def slot(q, par, buf, steady):
                t = 2 * q + par

                def mask_and_min(c):
                    if real(t, steady):
                        dve.wait_ge(s_done[c], t + 1)
                        dve.sem_inc(mask_turn, 1)
                        for j in range(HC):
                            s, h = scores[c][:, j * N:j * N + N], HC * c + j
                            last = nc.vector.tensor_tensor_reduce(
                                out=s, in0=s, in1=block_add[:], scale=-SCALE, scalar=HUGE, op0=ALU.add, op1=ALU.min,
                                accum_out=neg_max[:, par, h:h + 1])
                        last.then_inc(masked[c], 1)

                def invert_sums(c):
                    if real(t, steady):
                        dve.wait_ge(exp_done[c], t + 1)
                        heads = slice(HC * c, HC * c + HC)
                        nc.vector.reciprocal(row_inv[:, par, heads], row_sum[:, par, heads]).then_inc(inv_made[c], 1)

                if real(t - 2, steady):
                    o = pw_bank[:, 0:D]
                    dve.wait_ge(proj_done, t - 1)
                    nc.vector.bn_stats(o_raw[:, par], o).then_inc(o_stats, 1)
                    dve.wait_ge(x_added, q)
                    nc.vector.tensor_tensor(o_plus_x[:, par], o, x_plus_beta[:, bass.ds(t - 2, 1)].rearrange(
                        "p b d -> p (b d)"), ALU.add).then_inc(o_summed, 1)
                mask_and_min(0)
                if real(t - 2, steady):
                    dve.wait_ge(mask_made, 1)
                    dve.wait_ge(o_stats, t - 1)
                    nc.vector.bn_aggr(o_mv[:, par], o_raw[:, par]).then_inc(o_moments, 1)
                mask_and_min(1)
                if real(t - 2, steady):
                    dve.wait_ge(o_moments, t - 1)
                    nc.vector.scalar_tensor_tensor(o_gamma[:, par], o, o_mv[:, par, 0:1], gamma_b[:],
                                                   ALU.subtract, ALU.mult).then_inc(o_scaled, 1)
                if real(t - 4, steady):
                    dve.wait_ge(u_rstd_made, t - 3)
                    if steady or t - 6 >= 0:
                        dve.wait_ge(out_stored[par], 16 * (q - 2))
                    nc.vector.tensor_scalar(out_sb[:, par], u_sb[:, par], u_mv[:, par, 0:1], u_rstd[:, par],
                                            ALU.subtract, ALU.mult).then_inc(out_made, 1)
                invert_sums(0)
                if par == 0 and real_pair(q + 1, steady):
                    low_part(k_hi_made, q + 2, k_t[:, 1 - buf, 1], kv_bank[:].rearrange("p (c b m) -> p c b m", c=KC, b=2),
                             k_t[:, 1 - buf, 0], k_lo_made)
                if real(t - 3, steady):
                    low_part(yt_hi_made, t - 2, y_t_lo[:, 1 - par], oy_bank[:, 0:D].rearrange("p (c n) -> p c n", c=KC),
                             y_t_hi[:, 1 - par], yt_lo_made)
                if real(t - 2, steady):
                    dve.wait_ge(o_rstd_made, t - 1)
                    dve.wait_ge(o_scaled, t - 1)
                    dve.wait_ge(o_summed, t - 1)
                    nc.vector.scalar_tensor_tensor(t_sb[:, par], o_gamma[:, par], o_rstd[:, par], o_plus_x[:, par],
                                                   ALU.mult, ALU.add).then_inc(t_made, 1)
                    dve.wait_ge(t_made, t - 1)
                    nc.vector.bn_stats(t_raw[:, par], t_sb[:, par]).then_inc(t_stats, 1)
                if real(t - 3, steady):
                    dve.wait_ge(w_done, t - 2)
                    dve.wait_ge(x1_made, t - 2)
                    nc.vector.tensor_tensor(u_sb[:, 1 - par], pw_bank[:, 0:D], x1[:, 1 - par], ALU.add).then_inc(u_made, 1)
                if real(t - 2, steady):
                    dve.wait_ge(mask_made, 1)
                    dve.wait_ge(t_stats, t - 1)
                    nc.vector.bn_aggr(t_mv[:, par], t_raw[:, par]).then_inc(t_moments, 1)
                if real(t - 3, steady):
                    dve.wait_ge(u_made, t - 2)
                    nc.vector.bn_stats(u_raw[:, 1 - par], u_sb[:, 1 - par]).then_inc(u_stats, 1)
                if real(t - 1, steady):
                    low_part(ot_hi_made, t, o_t_lo[:, 1 - par], oy_bank[:, 0:D].rearrange("p (c n) -> p c n", c=KC),
                             o_t_hi[:, 1 - par], ot_lo_made)
                if real(t - 3, steady):
                    dve.wait_ge(mask_made, 1)
                    dve.wait_ge(u_stats, t - 2)
                    nc.vector.bn_aggr(u_mv[:, 1 - par], u_raw[:, 1 - par]).then_inc(u_moments, 1)
                if real(t - 2, steady):
                    dve.wait_ge(t_rstd_made, t - 1)
                    nc.vector.tensor_scalar(x1[:, par], t_sb[:, par], t_mv[:, par, 0:1], t_rstd[:, par],
                                            ALU.subtract, ALU.mult).then_inc(x1_made, 1)
                invert_sums(1)
                if par == 0 and real_pair(q + 1, steady):
                    low_part(q_hi_made, q + 2, q_t[:, 1 - buf, 1], qx_bank[:].rearrange("p (c b n) -> p c b n", c=KC, b=2),
                             q_t[:, 1 - buf, 0], q_lo_made)
                if par == 1 and real_pair(q + 2, steady):
                    low_part(xt_hi_made, q + 3, xt_lo[:, buf], qx_bank[:].rearrange("p (c b n) -> p c b n", c=KC, b=2),
                             xt_hi[:, buf], xt_lo_made)

            pair_slots(dve, slot)

        @block.tensor
        def _(pe):
            pe.wait_ge(ident_made, 1)
            pe.wait_ge(adj_in, 16)
            nc.tensor.transpose(trans[0][:, 0:N], adj_sb[:], ident[:]).then_inc(adjt_done, 1)

            def product(dest, parts_l, parts_r, start=True):
                terms = [(i, j, c) for i, j in ((0, 0), (0, 1), (1, 0)) for c in range(KC)]
                for n, (i, j, c) in enumerate(terms):
                    last = nc.tensor.matmul(dest, parts_l[i](c), parts_r[j](c), start=start and n == 0,
                                            stop=n == len(terms) - 1)
                return last

            def with_bias(n, parts_l, w_hi, w_lo):
                nc.tensor.matmul(pw_bank[:, 0:D], ones_r[:], bias_parts[:, n], start=True, stop=False)
                return product(pw_bank[:, 0:D], parts_l, [lambda c: w_hi[:, c], lambda c: w_lo[:, c]], start=False)

            def q_or_k(dest, first_col, buf):
                for m in range(KC):
                    cols = slice(first_col + 128 * m, first_col + 128 * m + 128)
                    last = product(dest[:, 2 * N * m:2 * N * m + 2 * N],
                                   [lambda c, w=w, cols=cols: w[:, c, cols] for w in (wqkv_hi, wqkv_lo)],
                                   [lambda c, xt=xt: xt[:, buf, c].rearrange("p b n -> p (b n)") for xt in (xt_hi, xt_lo)])
                return last

            def slot(q, par, buf, steady):
                t = 2 * q + par
                if real(t, steady):
                    pe.wait_ge(k_diag_in, 16 * HC * (q + 1))
                    pe.wait_ge(q_lo_made, q + 1)
                    for c in range(KC):
                        if steady or t >= 1:
                            pe.wait_ge(exp_done[c], t)
                        for i, j in ((0, 0), (0, 1), (1, 0)):
                            last = nc.tensor.matmul(scores[c][:], q_t[:, buf, i, c, par],
                                                    k_diag[:, buf, j, c, par].rearrange("p j m -> p (j m)"),
                                                    start=(i, j) == (0, 0), stop=i == 1)
                        last.then_inc(s_done[c], 1)
                if par == 0 and real_pair(q + 1, steady):
                    pe.wait_ge(xt_lo_made, q + 2)
                    if steady or q >= 0:
                        pe.wait_ge(v_made, q + 1)
                    q_or_k(kv_bank, D, 1 - buf).then_inc(k_done, 1)
                if par == 1 and real_pair(q + 1, steady):
                    pe.wait_ge(k_lo_made, q + 2)
                    for b in range(2):
                        last = product(kv_bank[:, D * b:D * b + D],
                                       [lambda c, xt=xt, b=b: xt[:, 1 - buf, c, b] for xt in (xt_hi, xt_lo)],
                                       [lambda c, w=w: w[:, c, 2 * D:3 * D] for w in (wqkv_hi, wqkv_lo)])
                    last.then_inc(v_done, 1)
                if real(t - 3, steady):
                    pe.wait_ge(x1_made, t - 2)
                    if steady or real(t - 2, False):
                        pe.wait_ge(ot_lo_made, t - 1)
                    for c in range(KC):
                        last = nc.tensor.matmul(oy_bank[:, c * N:c * N + N], x1[:, 1 - par, 128 * c:128 * c + 128],
                                                adj_t[:], start=True, stop=True)
                    last.then_inc(y_done, 1)
                if real(t - 1, steady):
                    for c in range(KC):
                        pe.wait_ge(normed[c], t)
                        if steady or t >= 2:
                            pe.wait_ge(pt_made[c], t - 1)
                        for j in range(HC):
                            last = nc.tensor.transpose(trans[c][:, j * N:j * N + N], probs[:, 1 - par, c, j], ident[:])
                        last.then_inc(pt_done[c], 1)
                if real(t - 3, steady):
                    pe.wait_ge(yt_lo_made, t - 2)
                    if steady or real(t - 2, False):
                        pe.wait_ge(o_scaled, t - 1)
                    with_bias(1, [lambda c: y_t_hi[:, 1 - par, c], lambda c: y_t_lo[:, 1 - par, c]],
                              wgnn_hi, wgnn_lo).then_inc(w_done, 1)
                if real(t - 1, steady):
                    pe.wait_ge(v_made, q + par)
                    if steady or real(t - 3, False):
                        pe.wait_ge(yt_lo_made, t - 2)
                    v = v_sb[:, buf if par else 1 - buf, 1 - par]
                    for c in range(KC):
                        pe.wait_ge(pt_made[c], t)
                        for j in range(HC):
                            first = 32 * (HC * c + j)
                            last = nc.tensor.matmul(oy_bank[32 * j:32 * j + 32, c * N:c * N + N],
                                                    v[:, first:first + 32], probs_t[:, 1 - par, c, j],
                                                    start=True, stop=True)
                    last.then_inc(pv_done, 1)
                if par == 0 and real_pair(q + 1, steady):
                    q_or_k(qx_bank, 0, 1 - buf).then_inc(q_done, 1)
                if par == 1 and real_pair(q + 2, steady):
                    pe.wait_ge(x_loaded, 16 * (q + 3))
                    if steady or q >= -1:
                        pe.wait_ge(q_lo_made, q + 2)
                    for c in range(KC):
                        for b in range(2):
                            at = (2 * c + b) * N
                            last = nc.tensor.transpose(qx_bank[:, at:at + N], x_in[:, b, 128 * c:128 * c + 128], ident[:])
                    last.then_inc(xt_done, 1)
                if real(t - 1, steady):
                    pe.wait_ge(ot_lo_made, t)
                    if steady or real(t - 3, False):
                        pe.wait_ge(u_made, t - 2)
                    with_bias(0, [lambda c: o_t_hi[:, 1 - par, c], lambda c: o_t_lo[:, 1 - par, c]],
                              wproj_hi, wproj_lo).then_inc(proj_done, 1)

            pe.wait_ge(ones_made, 1)
            pe.wait_ge(bias_made, 1)
            pe.wait_ge(lo_made, 3)
            pe.wait_ge(adjt_made, 1)
            pair_slots(pe, slot)


INPUTS = ["x", "adj", "L0_gnn_w_qkv", "L0_gnn_w_proj", "L0_gnn_b_proj", "L0_gnn_ln_gamma", "L0_gnn_ln_beta",
          "L1_gnn_weight", "L1_gnn_bias"]


def kernel(**inputs):
    import numpy as np
    import concourse.bacc as bacc
    from concourse.bass_utils import run_bass_kernel_spmd

    nc = bacc.Bacc("TRN2", target_bir_lowering=False, num_devices=1)
    arrays, args = {}, []
    for name in INPUTS:
        a = np.ascontiguousarray(inputs[name])
        arrays[f"in_{name}"] = a
        args.append(nc.dram_tensor(f"in_{name}", a.shape, mybir.dt.from_np(a.dtype), kind="ExternalInput").ap())
    args.append(nc.dram_tensor("result", inputs["x"].shape, F32, kind="ExternalOutput").ap())
    gnn_block_kernel(nc, *args)
    return run_bass_kernel_spmd(nc, [arrays], core_ids=[0]).results[0]["result"]
```

```python
import concourse.bass as bass
from concourse import mybir
from contextlib import ExitStack

F32 = mybir.dt.float32
F32R = mybir.dt.float32r
ALU = mybir.AluOpType
ACT = mybir.ActivationFunctionType


def gnn_block_kernel(nc, x, adj, w_qkv, w_proj, b_proj, gamma, beta, w_gnn, b_gnn, out):
    B, N, D = x.shape
    HD = 32
    H = D // HD
    KC = D // 128
    HC = H // KC
    PAIRS = B // 2
    SCALE = float(HD) ** -0.5
    EPS = 1e-5
    BLOCKED = -1e30
    HUGE = 3e38

    ctx = ExitStack()
    with ctx:
        def sb(name, shape, dt=F32):
            return ctx.enter_context(nc.sbuf_tensor(name, shape, dt))

        def bank(name):
            return ctx.enter_context(nc.psum_tensor(name, [128, 512], F32))

        def sem(name):
            return ctx.enter_context(nc.semaphore(name))

        wqkv = sb("wqkv", [128, KC, 3 * D])
        wqkv_hi = sb("wqkv_hi", [128, KC, 3 * D], F32R)
        wqkv_lo = sb("wqkv_lo", [128, KC, 3 * D], F32R)
        wproj, wgnn = sb("wproj", [128, KC, D]), sb("wgnn", [128, KC, D])
        wproj_hi, wproj_lo = sb("wproj_hi", [128, KC, D], F32R), sb("wproj_lo", [128, KC, D], F32R)
        wgnn_hi, wgnn_lo = sb("wgnn_hi", [128, KC, D], F32R), sb("wgnn_lo", [128, KC, D], F32R)
        gamma_b = sb("gamma_b", [128, D])
        beta_b = sb("beta_b", [128, D])
        b_gnn_b = sb("b_gnn_b", [128, D])
        bias_rows = sb("bias_rows", [128, D])
        bias_hi = sb("bias_hi", [128, D], F32R)
        bias_lo = sb("bias_lo", [128, D])
        bias_parts = sb("bias_parts", [128, D], F32R)
        ones_f = sb("ones_f", [128, 128])
        ones_r = sb("ones_r", [128, 128], F32R)
        ident = sb("ident", [128, 128])
        adj_sb = sb("adj_sb", [128, N])
        adj_t = sb("adj_t", [128, N])
        block_add = sb("block_add", [128, N])
        minus_half, eps_col, minus_one = (sb(n, [128, 1]) for n in ("minus_half", "eps_col", "minus_one"))

        x_in = sb("x_in", [128, 2, D])
        xt_hi = sb("xt_hi", [128, 2, KC, 2, N], F32R)
        xt_lo = sb("xt_lo", [128, 2, KC, 2, N], F32R)
        q_t = sb("q_t", [128, 2, 2, KC, 2, N], F32R)
        k_t = sb("k_t", [128, 2, 2, KC, 2, N], F32R)
        k_diag = sb("k_diag", [128, 2, 2, KC, 2, HC, N], F32R)
        v_sb = sb("v_sb", [128, 2, 2, D])
        x_plus_beta = sb("x_plus_beta", [128, B, D])
        probs = sb("probs", [128, 2, KC, HC, N])
        neg_max = sb("neg_max", [128, 2, H])
        row_sum = sb("row_sum", [128, 2, H])
        row_inv = sb("row_inv", [128, 2, H])
        probs_t = sb("probs_t", [128, 2, KC, HC, N])
        o_t_hi, o_t_lo = sb("o_t_hi", [128, 2, KC, N], F32R), sb("o_t_lo", [128, 2, KC, N], F32R)
        o_gamma = sb("o_gamma", [128, 2, D])
        o_plus_x = sb("o_plus_x", [128, 2, D])
        t_sb = sb("t_sb", [128, 2, D])
        x1, x1_bias = sb("x1", [128, 2, D]), sb("x1_bias", [128, 2, D])
        y_t_hi, y_t_lo = sb("y_t_hi", [128, 2, KC, N], F32R), sb("y_t_lo", [128, 2, KC, N], F32R)
        u_sb = sb("u_sb", [128, 2, D])
        out_sb = sb("out_sb", [128, 2, D])
        o_raw, t_raw, u_raw = (sb(n, [128, 2, 6]) for n in ("o_raw", "t_raw", "u_raw"))
        o_mv, t_mv, u_mv = (sb(n, [128, 2, 2]) for n in ("o_mv", "t_mv", "u_mv"))
        o_ve, t_ve, u_ve = (sb(n, [128, 2, 1]) for n in ("o_ve", "t_ve", "u_ve"))
        o_rstd, t_rstd, u_rstd = (sb(n, [128, 2, 1]) for n in ("o_rstd", "t_rstd", "u_rstd"))
        u_shift = sb("u_shift", [128, 2, 1])

        scores = [bank("scores0"), bank("scores1")]
        trans = [bank("trans0"), bank("trans1")]
        kv_bank, qx_bank = bank("kv_bank"), bank("qx_bank")
        oy_bank, pw_bank = bank("oy_bank"), bank("pw_bank")

        x_loaded, k_diag_in = sem("x_loaded"), sem("k_diag_in")
        out_stored = [sem("out_stored0"), sem("out_stored1")]
        wk_in, wq_in, wv_in = sem("wk_in"), sem("wq_in"), sem("wv_in")
        adj_in, bias_in, beta_in = sem("adj_in"), sem("bias_in"), sem("beta_in")
        b_gnn_in = sem("b_gnn_in")
        gamma_in, wproj_in, wgnn_in = sem("gamma_in"), sem("wproj_in"), sem("wgnn_in")
        bias_zero, ident_zero, ident_made, kdiag_zero = (
            sem("bias_zero"), sem("ident_zero"), sem("ident_made"), sem("kdiag_zero"))
        half_made, hi_made, lo_made, bias_step = sem("half_made"), sem("hi_made"), sem("lo_made"), sem("bias_step")
        bias_made, ones_set, ones_made = sem("bias_made"), sem("ones_set"), sem("ones_made")
        adjt_done, adjt_made, mask_made = sem("adjt_done"), sem("adjt_made"), sem("mask_made")
        carries_wait = sem("carries_wait")
        xt_done, xt_hi_made, xt_lo_made = sem("xt_done"), sem("xt_hi_made"), sem("xt_lo_made")
        k_done, k_hi_made, k_lo_made = sem("k_done"), sem("k_hi_made"), sem("k_lo_made")
        q_done, q_hi_made, q_lo_made = sem("q_done"), sem("q_hi_made"), sem("q_lo_made")
        v_done, v_made, x_added = sem("v_done"), sem("v_made"), sem("x_added")
        s_done = [sem("s_done0"), sem("s_done1")]
        masked = [sem("masked0"), sem("masked1")]
        exp_done = [sem("exp_done0"), sem("exp_done1")]
        inv_made = [sem("inv_made0"), sem("inv_made1")]
        normed = [sem("normed0"), sem("normed1")]
        pt_done = [sem("pt_done0"), sem("pt_done1")]
        pt_made = [sem("pt_made0"), sem("pt_made1")]
        pv_done, ot_hi_made, ot_lo_made, proj_done = (
            sem("pv_done"), sem("ot_hi_made"), sem("ot_lo_made"), sem("proj_done"))
        o_stats, o_moments, o_scaled, o_summed = sem("o_stats"), sem("o_moments"), sem("o_scaled"), sem("o_summed")
        o_eps, o_rstd_made = sem("o_eps"), sem("o_rstd_made")
        t_made, t_stats, t_moments, t_eps, t_rstd_made = (
            sem("t_made"), sem("t_stats"), sem("t_moments"), sem("t_eps"), sem("t_rstd_made"))
        x1_biased = sem("x1_biased")
        x1_made, y_done, yt_hi_made, yt_lo_made, w_done = (
            sem("x1_made"), sem("y_done"), sem("yt_hi_made"), sem("yt_lo_made"), sem("w_done"))
        u_made, u_stats, u_moments, u_eps, u_rstd_made = (
            sem("u_made"), sem("u_stats"), sem("u_moments"), sem("u_eps"), sem("u_rstd_made"))
        u_mean_scaled, u_shift_made, out_made = sem("u_mean_scaled"), sem("u_shift_made"), sem("out_made")

        def pair_slots(eng, slot):
            FIRST, LAST = 2, PAIRS // 2 - 2

            def pair(q, buf, steady):
                slot(q, 0, buf, steady)
                slot(q, 1, buf, steady)

            for q in range(-4, 2 * FIRST):
                pair(q, q % 2, False)
            with eng.Fori(FIRST, LAST) as r:
                pair(2 * r, 0, True)
                pair(2 * r + 1, 1, True)
            for q in range(2 * LAST, PAIRS + 5):
                pair(q, q % 2, False)

        def real(b, steady):
            return steady or 0 <= b < B

        def real_pair(q, steady):
            return steady or 0 <= q < PAIRS

        block = ctx.enter_context(nc.Block())

        @block.sync
        def _(sp):
            sp.dma_start(x_in[:], x[0:2].rearrange("b n d -> n b d")).then_inc(x_loaded, 16)
            for n, loaded in ((1, wk_in), (0, wq_in), (2, wv_in)):
                sp.dma_start(wqkv[:, :, n * D:n * D + D], w_qkv.rearrange("(c p) e -> p c e", p=128)[:, :, n * D:n * D + D]
                             ).then_inc(loaded, 16)
                if n == 1:
                    sp.dma_start(adj_sb[:], adj).then_inc(adj_in, 16)
                    sp.dma_start(beta_b[:], beta.partition_broadcast(128)).then_inc(beta_in, 16)
            sp.dma_start(wproj[:], w_proj.rearrange("(c p) e -> p c e", p=128)).then_inc(wproj_in, 16)
            sp.dma_start(wgnn[:], w_gnn.rearrange("(c p) e -> p c e", p=128)).then_inc(wgnn_in, 16)
            sp.wait_ge(bias_zero, 1)
            sp.dma_start(bias_rows[0:2, :], b_proj.partition_broadcast(2)).then_inc(bias_in, 16)
            sp.dma_start(gamma_b[:], gamma.partition_broadcast(128)).then_inc(gamma_in, 16)
            sp.dma_start(b_gnn_b[:], b_gnn.partition_broadcast(128)).then_inc(b_gnn_in, 16)

            def slot(q, par, buf, steady):
                t = 2 * q + par
                if par == 0 and real_pair(q + 1, steady):
                    sp.wait_ge(kdiag_zero, 2 if steady or q >= 0 else 1)
                    sp.wait_ge(k_lo_made, q + 2)
                    for g in range(HC):
                        rows = slice(32 * g, 32 * g + 32)
                        sp.dma_start(
                            k_diag[rows, 1 - buf, :, :, :, g, :].bitcast(F32).rearrange("p i c b m -> p (i c b) m"),
                            k_t[rows, 1 - buf].bitcast(F32).rearrange("p i c b m -> p (i c b) m")).then_inc(k_diag_in, 16)
                if par == 1 and (steady or 1 <= q + 3 < PAIRS):
                    if real_pair(q + 2, steady):
                        sp.wait_ge(xt_done, q + 3)
                        sp.wait_ge(x_added, q + 3)
                    sp.dma_start(x_in[:], x[bass.ds(2 * q + 6, 2)].rearrange("b n d -> n b d")).then_inc(x_loaded, 16)
                if real(t - 6, steady):
                    sp.wait_ge(out_made, t - 5)
                    sp.dma_start(out[bass.ds(t - 6, 1)].rearrange("b n d -> n (b d)"),
                                 out_sb[:, par]).then_inc(out_stored[par], 16)

            pair_slots(sp, slot)
            for par in range(2):
                sp.wait_ge(out_stored[par], 16 * PAIRS)

        @block.gpsimd
        def _(pool):
            def add_beta(first):
                nc.gpsimd.tensor_tensor(
                    x_plus_beta[:, bass.ds(first, 2)], x_in[:],
                    beta_b[:, None, :].to_broadcast([128, 2, D]), ALU.add).then_inc(x_added, 1)

            nc.gpsimd.memset(ident[:], 0.0).then_inc(ident_zero, 1)
            pool.wait_ge(ident_zero, 1)
            nc.gpsimd.affine_select(out=ident[:], in_=ident[:], compare_op=ALU.not_equal, fill=1.0, base=0,
                                    pattern=[[-1, 128]], channel_multiplier=1).then_inc(ident_made, 1)
            nc.gpsimd.memset(bias_rows[:], 0.0).then_inc(bias_zero, 1)
            for n in range(2):
                nc.gpsimd.memset(k_diag[:, n].bitcast(F32), 0.0).then_inc(kdiag_zero, 1)
                if n == 0:
                    nc.gpsimd.memset(minus_half[:], -0.5).then_inc(half_made, 1)
                    nc.gpsimd.memset(eps_col[:], EPS).then_inc(half_made, 1)
                    nc.gpsimd.memset(minus_one[:], -1.0).then_inc(half_made, 1)
                    pool.wait_ge(half_made, 3)
                    pool.wait_ge(beta_in, 16)
                    pool.wait_ge(x_loaded, 16)
                    add_beta(0)
            pool.wait_ge(b_gnn_in, 16)

            def rstd(count, par, mv, with_eps, eps_made, dest, made):
                nc.gpsimd.tensor_tensor(with_eps[:, par], mv[:, par, 1:2], eps_col[:], ALU.add).then_inc(eps_made, 1)
                pool.wait_ge(eps_made, count)
                nc.gpsimd.tensor_tensor(dest[:, par], with_eps[:, par], minus_half[:], ALU.pow).then_inc(made, 1)

            def normalise(c, par):
                p = probs[:, par, c]
                nc.gpsimd.tensor_tensor(
                    p, p, row_inv[:, par, HC * c:HC * c + HC, None].to_broadcast([128, HC, N]),
                    ALU.mult).then_inc(normed[c], 1)

            def slot(q, par, buf, steady):
                t = 2 * q + par
                if real(t, steady):
                    pool.wait_ge(inv_made[0], t + 1)
                    normalise(0, par)
                    pool.wait_ge(inv_made[1], t + 1)
                    normalise(1, par)
                if real(t - 2, steady):
                    pool.wait_ge(t_moments, t - 1)
                    rstd(t - 1, par, t_mv, t_ve, t_eps, t_rstd, t_rstd_made)
                if par == 1 and (steady or 1 <= q + 3 < PAIRS):
                    pool.wait_ge(x_loaded, 16 * (q + 4))
                    add_beta(2 * q + 6)
                if real(t - 4, steady):
                    pool.wait_ge(u_moments, t - 3)
                    rstd(t - 3, par, u_mv, u_ve, u_eps, u_rstd, u_rstd_made)
                if real(t - 2, steady):
                    pool.wait_ge(x1_made, t - 1)
                    nc.gpsimd.tensor_tensor(x1_bias[:, par], x1[:, par], b_gnn_b[:], ALU.add).then_inc(x1_biased, 1)
                if real(t - 4, steady):
                    pool.wait_ge(u_rstd_made, t - 3)
                    nc.gpsimd.tensor_tensor(u_shift[:, par], u_mv[:, par, 0:1], u_rstd[:, par],
                                            ALU.mult).then_inc(u_mean_scaled, 1)
                    pool.wait_ge(u_mean_scaled, t - 3)
                    nc.gpsimd.tensor_tensor(u_shift[:, par], u_shift[:, par], minus_one[:],
                                            ALU.mult).then_inc(u_shift_made, 1)
                if real(t - 1, steady):
                    pool.wait_ge(o_moments, t)
                    rstd(t, 1 - par, o_mv, o_ve, o_eps, o_rstd, o_rstd_made)

            pair_slots(pool, slot)

        @block.scalar
        def _(act):
            def high_part(hi, w, loaded):
                act.wait_ge(loaded, 16)
                nc.scalar.activation(hi, w, ACT.Copy).then_inc(hi_made, 1)

            high_part(wqkv_hi[:, :, D:2 * D], wqkv[:, :, D:2 * D], wk_in)

            def other_constants():
                high_part(wqkv_hi[:, :, 0:D], wqkv[:, :, 0:D], wq_in)
                high_part(wqkv_hi[:, :, 2 * D:3 * D], wqkv[:, :, 2 * D:3 * D], wv_in)
                high_part(wproj_hi[:], wproj[:], wproj_in)
                high_part(wgnn_hi[:], wgnn[:], wgnn_in)
                act.wait_ge(adjt_done, 1)
                nc.scalar.activation(adj_t[:], trans[0][:, 0:N], ACT.Copy).then_inc(adjt_made, 1)

            def exps(c, par, heads=range(HC)):
                for j in heads:
                    h = HC * c + j
                    last = nc.scalar.activation(
                        probs[:, par, c, j], scores[c][:, j * N:j * N + N], ACT.Exp,
                        bias=neg_max[:, par, h:h + 1], scale=-1.0, accum_out=row_sum[:, par, h:h + 1])
                return last

            def slot(q, par, buf, steady):
                t = 2 * q + par
                if not steady and (q, par) == (-1, 0):
                    other_constants()
                if real(t - 2, steady):
                    act.wait_ge(pt_done[0], t - 1)
                    nc.scalar.activation(probs_t[:, par, 0], trans[0][:].rearrange("p (j n) -> p j n", j=HC),
                                         ACT.Copy).then_inc(pt_made[0], 1)
                if real(t - 4, steady):
                    act.wait_ge(y_done, t - 3)
                    nc.scalar.activation(y_t_hi[:, par], oy_bank[:, 0:D].rearrange("p (c n) -> p c n", c=KC),
                                         ACT.Copy).then_inc(yt_hi_made, 1)
                if real(t - 2, steady):
                    act.wait_ge(pt_done[1], t - 1)
                    nc.scalar.activation(probs_t[:, par, 1], trans[1][:].rearrange("p (j n) -> p j n", j=HC),
                                         ACT.Copy).then_inc(pt_made[1], 1)
                if real(t, steady):
                    act.wait_ge(masked[0], t + 1)
                    exps(0, par).then_inc(exp_done[0], 1)
                if par == 0 and real_pair(q + 1, steady):
                    act.wait_ge(k_done, q + 2)
                    nc.scalar.activation(k_t[:, 1 - buf, 0], kv_bank[:].rearrange("p (c b n) -> p c b n", c=KC, b=2),
                                         ACT.Copy).then_inc(k_hi_made, 1)
                if real(t - 6, steady):
                    act.wait_ge(u_shift_made, t - 5)
                    if real(t - 8, steady):
                        act.wait_ge(out_stored[par], 16 * (q - 3))
                    nc.scalar.activation(out_sb[:, par], u_sb[:, par], ACT.Identity, bias=u_shift[:, par],
                                         scale=u_rstd[:, par]).then_inc(out_made, 1)
                if real(t - 2, steady):
                    act.wait_ge(pv_done, t - 1)
                    nc.scalar.activation(o_t_hi[:, par], oy_bank[:, 0:D].rearrange("p (c n) -> p c n", c=KC),
                                         ACT.Copy).then_inc(ot_hi_made, 1)
                if par == 1 and real_pair(q + 1, steady):
                    act.wait_ge(v_done, q + 2)
                    nc.scalar.activation(v_sb[:, 1 - buf], kv_bank[:].rearrange("p (b d) -> p b d", b=2),
                                         ACT.Copy).then_inc(v_made, 1)
                if par == 0 and real_pair(q + 1, steady):
                    act.wait_ge(q_done, q + 2)
                    nc.scalar.activation(q_t[:, 1 - buf, 0], qx_bank[:].rearrange("p (c b n) -> p c b n", c=KC, b=2),
                                         ACT.Copy).then_inc(q_hi_made, 1)
                if par == 1 and real_pair(q + 2, steady):
                    act.wait_ge(xt_done, q + 3)
                    nc.scalar.activation(xt_hi[:, buf], qx_bank[:].rearrange("p (c b n) -> p c b n", c=KC, b=2),
                                         ACT.Copy).then_inc(xt_hi_made, 1)
                if real(t, steady):
                    act.wait_ge(masked[1], t + 1)
                    exps(1, par).then_inc(exp_done[1], 1)

            pair_slots(act, slot)

        @block.vector
        def _(dve):
            nc.vector.memset(ones_f[:], 1.0).then_inc(ones_set, 1)
            dve.wait_ge(ones_set, 1)
            nc.vector.tensor_copy(ones_r[:], ones_f[:]).then_inc(ones_made, 1)
            def weights_low_part(n, lo, w, hi):
                dve.wait_ge(hi_made, n)
                nc.vector.tensor_tensor(lo, w, hi.bitcast(F32), ALU.subtract).then_inc(lo_made, 1)

            wk, wq, wv = slice(D, 2 * D), slice(0, D), slice(2 * D, 3 * D)
            weights_low_part(1, wqkv_lo[:, :, wk], wqkv[:, :, wk], wqkv_hi[:, :, wk])

            def other_constants():
                weights_low_part(2, wqkv_lo[:, :, wq], wqkv[:, :, wq], wqkv_hi[:, :, wq])
                weights_low_part(3, wqkv_lo[:, :, wv], wqkv[:, :, wv], wqkv_hi[:, :, wv])
                weights_low_part(4, wproj_lo[:], wproj[:], wproj_hi[:])
                weights_low_part(5, wgnn_lo[:], wgnn[:], wgnn_hi[:])

            def mask_and_bias():
                dve.wait_ge(adj_in, 16)
                nc.vector.tensor_scalar(block_add[:], adj_sb[:], 0.0, BLOCKED, ALU.is_equal, ALU.mult).then_inc(mask_made, 1)
                dve.wait_ge(bias_in, 16)
                nc.vector.tensor_copy(bias_hi[:], bias_rows[:]).then_inc(bias_step, 1)
                dve.wait_ge(bias_step, 1)
                nc.vector.tensor_tensor(bias_lo[:], bias_rows[:], bias_hi[:].bitcast(F32), ALU.subtract).then_inc(bias_step, 1)
                dve.wait_ge(bias_step, 2)
                dve.wait_ge(ident_made, 1)
                nc.vector.tensor_scalar(bias_lo[:], bias_lo[:], ident[:, 1:2], None, ALU.mult).then_inc(bias_step, 1)
                dve.wait_ge(bias_step, 3)
                nc.vector.scalar_tensor_tensor(bias_parts[:], bias_hi[:].bitcast(F32), ident[:, 0:1],
                                               bias_lo[:], ALU.mult, ALU.add).then_inc(bias_made, 1)
                dve.wait_ge(mask_made, 1)
                dve.wait_ge(gamma_in, 16)

            heads = [slice(HC * c, HC * c + HC) for c in range(KC)]

            def low_part(low, full, high, low_made):
                nc.vector.tensor_tensor(low, full, high.bitcast(F32), ALU.subtract).then_inc(low_made, 1)

            def mask_and_min(c, par):
                dve.sem_inc(carries_wait, 1)
                for j in range(HC):
                    s, h = scores[c][:, j * N:j * N + N], HC * c + j
                    last = nc.vector.tensor_tensor_reduce(
                        out=s, in0=s, in1=block_add[:], scale=-SCALE, scalar=HUGE, op0=ALU.add, op1=ALU.min,
                        accum_out=neg_max[:, par, h:h + 1])
                last.then_inc(masked[c], 1)

            def slot(q, par, buf, steady):
                t = 2 * q + par
                if not steady and (q, par) == (-1, 1):
                    other_constants()
                if not steady and (q, par) == (0, 0):
                    mask_and_bias()
                if real(t - 4, steady):
                    dve.wait_ge(t_stats, t - 3)
                    dve.sem_inc(carries_wait, 1)
                    nc.vector.bn_aggr(t_mv[:, par], t_raw[:, par]).then_inc(t_moments, 1)
                if par == 1 and real_pair(q + 1, steady):
                    dve.wait_ge(k_hi_made, q + 2)
                    low_part(k_t[:, 1 - buf, 1], kv_bank[:].rearrange("p (c b n) -> p c b n", c=KC, b=2), k_t[:, 1 - buf, 0], k_lo_made)
                if real(t - 6, steady):
                    dve.wait_ge(u_stats, t - 5)
                    dve.sem_inc(carries_wait, 1)
                    nc.vector.bn_aggr(u_mv[:, par], u_raw[:, par]).then_inc(u_moments, 1)
                if real(t - 3, steady):
                    dve.wait_ge(ot_hi_made, t - 2)
                    low_part(o_t_lo[:, 1 - par], oy_bank[:, 0:D].rearrange("p (c n) -> p c n", c=KC),
                             o_t_hi[:, 1 - par], ot_lo_made)
                if real(t - 5, steady):
                    dve.wait_ge(w_done, t - 4)
                    if real(t - 7, steady):
                        dve.wait_ge(out_made, t - 6)
                    nc.vector.tensor_tensor(u_sb[:, 1 - par], pw_bank[:, 0:D], x1_bias[:, 1 - par], ALU.add).then_inc(u_made, 1)
                if par == 0 and real_pair(q + 1, steady):
                    dve.wait_ge(xt_hi_made, q + 2)
                    low_part(xt_lo[:, 1 - buf], qx_bank[:].rearrange("p (c b n) -> p c b n", c=KC, b=2), xt_hi[:, 1 - buf], xt_lo_made)
                if real(t - 4, steady):
                    dve.wait_ge(t_rstd_made, t - 3)
                    nc.vector.tensor_scalar(x1[:, par], t_sb[:, par], t_mv[:, par, 0:1], t_rstd[:, par],
                                            ALU.subtract, ALU.mult).then_inc(x1_made, 1)
                if real(t, steady):
                    dve.wait_ge(s_done[0], t + 1)
                    mask_and_min(0, par)
                if par == 1 and real_pair(q + 1, steady):
                    dve.wait_ge(q_hi_made, q + 2)
                    low_part(q_t[:, 1 - buf, 1], qx_bank[:].rearrange("p (c b n) -> p c b n", c=KC, b=2), q_t[:, 1 - buf, 0], q_lo_made)
                if real(t - 3, steady):
                    dve.wait_ge(proj_done, t - 2)
                    nc.vector.bn_stats(o_raw[:, 1 - par], pw_bank[:, 0:D]).then_inc(o_stats, 1)
                if real(t - 1, steady):
                    nc.vector.reciprocal(row_inv[:, 1 - par, heads[0]], row_sum[:, 1 - par, heads[0]]).then_inc(inv_made[0], 1)
                    dve.wait_ge(exp_done[1], t)
                    nc.vector.reciprocal(row_inv[:, 1 - par, heads[1]], row_sum[:, 1 - par, heads[1]]).then_inc(inv_made[1], 1)
                if real(t - 3, steady):
                    dve.wait_ge(o_stats, t - 2)
                    dve.sem_inc(carries_wait, 1)
                    nc.vector.bn_aggr(o_mv[:, 1 - par], o_raw[:, 1 - par]).then_inc(o_moments, 1)
                    nc.vector.tensor_tensor(o_plus_x[:, 1 - par], pw_bank[:, 0:D],
                                            x_plus_beta[:, bass.ds(t - 3, 1)].rearrange("p b d -> p (b d)"),
                                            ALU.add).then_inc(o_summed, 1)
                    dve.wait_ge(o_moments, t - 2)
                    nc.vector.scalar_tensor_tensor(o_gamma[:, 1 - par], pw_bank[:, 0:D], o_mv[:, 1 - par, 0:1], gamma_b[:],
                                                   ALU.subtract, ALU.mult).then_inc(o_scaled, 1)
                if real(t - 4, steady):
                    dve.wait_ge(yt_hi_made, t - 3)
                    low_part(y_t_lo[:, par], oy_bank[:, 0:D].rearrange("p (c n) -> p c n", c=KC),
                             y_t_hi[:, par], yt_lo_made)
                if real(t - 3, steady):
                    dve.wait_ge(o_rstd_made, t - 2)
                    dve.wait_ge(o_scaled, t - 2)
                    nc.vector.scalar_tensor_tensor(t_sb[:, 1 - par], o_gamma[:, 1 - par], o_rstd[:, 1 - par], o_plus_x[:, 1 - par],
                                                   ALU.mult, ALU.add).then_inc(t_made, 1)
                if real(t - 5, steady):
                    dve.wait_ge(u_made, t - 4)
                    nc.vector.bn_stats(u_raw[:, 1 - par], u_sb[:, 1 - par]).then_inc(u_stats, 1)
                if real(t - 3, steady):
                    dve.wait_ge(t_made, t - 2)
                    nc.vector.bn_stats(t_raw[:, 1 - par], t_sb[:, 1 - par]).then_inc(t_stats, 1)
                if real(t, steady):
                    dve.wait_ge(s_done[1], t + 1)
                    mask_and_min(1, par)

            pair_slots(dve, slot)

        @block.tensor
        def _(pe):
            pe.wait_ge(ident_made, 1)

            def warm_up(count):
                for n in range(count):
                    nc.tensor.transpose(trans[1][:, 0:128], ident[:], ident[:])

            warm_up(8)

            def transpose_adj():
                warm_up(6)
                pe.wait_ge(adj_in, 16)
                nc.tensor.transpose(trans[0][:, 0:N], adj_sb[:], ident[:]).then_inc(adjt_done, 1)

            def product(dest, parts_l, parts_r, start=True):
                terms = [(i, j, c) for i, j in ((0, 0), (0, 1), (1, 0)) for c in range(KC)]
                for n, (i, j, c) in enumerate(terms):
                    last = nc.tensor.matmul(dest, parts_l[i](c), parts_r[j](c), start=start and n == 0,
                                            stop=n == len(terms) - 1)
                return last

            def q_or_k(dest, first_col, buf):
                for m in range(KC):
                    cols = slice(first_col + 128 * m, first_col + 128 * m + 128)
                    last = product(dest[:, 2 * N * m:2 * N * m + 2 * N],
                                   [lambda c, w=w, cols=cols: w[:, c, cols] for w in (wqkv_hi, wqkv_lo)],
                                   [lambda c, xt=xt: xt[:, buf, c].rearrange("p b n -> p (b n)") for xt in (xt_hi, xt_lo)])
                return last

            def scores_of(c, buf, par):
                for i, j in ((0, 0), (0, 1), (1, 0)):
                    last = nc.tensor.matmul(scores[c][:], q_t[:, buf, i, c, par],
                                            k_diag[:, buf, j, c, par].rearrange("p j m -> p (j m)"),
                                            start=(i, j) == (0, 0), stop=i == 1)
                return last

            def slot(q, par, buf, steady):
                t = 2 * q + par
                if not steady and (q, par) == (-1, 0):
                    transpose_adj()
                if not steady and (q, par) == (0, 0):
                    warm_up(16)
                if real(t, steady):
                    pe.wait_ge(k_diag_in, 16 * HC * (q + 1))
                    if real(t - 1, steady):
                        pe.wait_ge(exp_done[0], t)
                    scores_of(0, buf, par).then_inc(s_done[0], 1)
                if real(t - 2, steady):
                    pe.wait_ge(normed[0], t - 1)
                    for j in range(HC):
                        last = nc.tensor.transpose(trans[0][:, j * N:j * N + N], probs[:, par, 0, j], ident[:])
                    last.then_inc(pt_done[0], 1)
                if real(t - 3, steady):
                    if not steady:
                        pe.wait_ge(lo_made, 4)
                        pe.wait_ge(ones_made, 1)
                        pe.wait_ge(bias_made, 1)
                    pe.wait_ge(ot_lo_made, t - 2)
                    if real(t - 5, steady):
                        pe.wait_ge(u_made, t - 4)
                    nc.tensor.matmul(pw_bank[:, 0:D], ones_r[:], bias_parts[:], start=True, stop=False)
                    product(pw_bank[:, 0:D], [lambda c: o_t_hi[:, 1 - par, c], lambda c: o_t_lo[:, 1 - par, c]],
                            [lambda c: wproj_hi[:, c], lambda c: wproj_lo[:, c]], start=False).then_inc(proj_done, 1)
                if real(t - 2, steady):
                    pe.wait_ge(normed[1], t - 1)
                    for j in range(HC):
                        last = nc.tensor.transpose(trans[1][:, j * N:j * N + N], probs[:, par, 1, j], ident[:])
                    last.then_inc(pt_done[1], 1)
                if real(t - 4, steady):
                    if not steady:
                        pe.wait_ge(adjt_made, 1)
                    pe.wait_ge(x1_made, t - 3)
                    for c in range(KC):
                        last = nc.tensor.matmul(oy_bank[:, c * N:c * N + N], x1[:, par, 128 * c:128 * c + 128],
                                                adj_t[:], start=True, stop=True)
                    last.then_inc(y_done, 1)
                if par == 0 and real_pair(q + 1, steady):
                    if not steady:
                        pe.wait_ge(lo_made, 1)
                    pe.wait_ge(xt_lo_made, q + 2)
                    q_or_k(kv_bank, D, 1 - buf).then_inc(k_done, 1)
                if par == 1 and real_pair(q + 1, steady):
                    if not steady:
                        pe.wait_ge(lo_made, 3)
                    pe.wait_ge(k_lo_made, q + 2)
                    for b in range(2):
                        last = product(kv_bank[:, D * b:D * b + D],
                                       [lambda c, xt=xt, b=b: xt[:, 1 - buf, c, b] for xt in (xt_hi, xt_lo)],
                                       [lambda c, w=w: w[:, c, 2 * D:3 * D] for w in (wqkv_hi, wqkv_lo)])
                    last.then_inc(v_done, 1)
                if real(t, steady):
                    if real(t - 1, steady):
                        pe.wait_ge(exp_done[1], t)
                    scores_of(1, buf, par).then_inc(s_done[1], 1)
                if real(t - 2, steady):
                    pe.wait_ge(pt_made[1], t - 1)
                    if real(t - 4, steady):
                        pe.wait_ge(yt_lo_made, t - 3)
                    v = v_sb[:, 1 - buf, par]
                    for c in range(KC):
                        for j in range(HC):
                            first = 32 * (HC * c + j)
                            last = nc.tensor.matmul(oy_bank[32 * j:32 * j + 32, c * N:c * N + N],
                                                    v[:, first:first + 32], probs_t[:, par, c, j],
                                                    start=True, stop=True)
                    last.then_inc(pv_done, 1)
                if par == 1 and real_pair(q + 2, steady):
                    pe.wait_ge(x_loaded, 16 * (q + 3))
                    if real_pair(q + 1, steady):
                        pe.wait_ge(q_lo_made, q + 2)
                    for c in range(KC):
                        for b in range(2):
                            at = (2 * c + b) * N
                            last = nc.tensor.transpose(qx_bank[:, at:at + N], x_in[:, b, 128 * c:128 * c + 128], ident[:])
                    last.then_inc(xt_done, 1)
                if real(t - 4, steady):
                    if not steady:
                        pe.wait_ge(lo_made, 5)
                    pe.wait_ge(yt_lo_made, t - 3)
                    product(pw_bank[:, 0:D], [lambda c: y_t_hi[:, par, c], lambda c: y_t_lo[:, par, c]],
                            [lambda c: wgnn_hi[:, c], lambda c: wgnn_lo[:, c]]).then_inc(w_done, 1)
                if par == 0 and real_pair(q + 1, steady):
                    if not steady:
                        pe.wait_ge(lo_made, 2)
                    q_or_k(qx_bank, 0, 1 - buf).then_inc(q_done, 1)

            pair_slots(pe, slot)


INPUTS = ["x", "adj", "L0_gnn_w_qkv", "L0_gnn_w_proj", "L0_gnn_b_proj", "L0_gnn_ln_gamma", "L0_gnn_ln_beta",
          "L1_gnn_weight", "L1_gnn_bias"]


def kernel(**inputs):
    import numpy as np
    import concourse.bacc as bacc
    from concourse.bass_utils import run_bass_kernel_spmd

    nc = bacc.Bacc("TRN2", target_bir_lowering=False, num_devices=1)
    arrays, args = {}, []
    for name in INPUTS:
        a = np.ascontiguousarray(inputs[name])
        arrays[f"in_{name}"] = a
        args.append(nc.dram_tensor(f"in_{name}", a.shape, mybir.dt.from_np(a.dtype), kind="ExternalInput").ap())
    args.append(nc.dram_tensor("result", inputs["x"].shape, F32, kind="ExternalOutput").ap())
    gnn_block_kernel(nc, *args)
    return run_bass_kernel_spmd(nc, [arrays], core_ids=[0]).results[0]["result"]
```
